# Optimizing a Trainium2 kernel written in Bass

```python
import numpy as np
import jax
import jax.numpy as jnp

def _softmax(x, axis=-1):
    return jax.nn.softmax(x, axis=axis)

def _gelu(x):
    return jax.nn.gelu(x, approximate=True)

def _silu(x):
    return jax.nn.silu(x)

def _sigmoid(x):
    return jax.nn.sigmoid(x)

def _layernorm(x, axis=-1, eps=1e-05):
    m = jnp.mean(x, axis=axis, keepdims=True)
    v = jnp.var(x, axis=axis, keepdims=True)
    return (x - m) / jnp.sqrt(v + eps)

def _scatter_add(tgt, idx, src, axis=0):
    return tgt.at[idx].add(src)

def _segment_sum(src, seg, n):
    return jax.ops.segment_sum(src, seg, n)
kernel_name = 'mk_conv_attn_hybrid_d2_conv_nhwc512_r4_12e8d4'

def setup_inputs(seed: int=0):
    np.random.seed(seed)
    _w = jnp.asarray

    def _rec_inputs():
        import jax
        import jax.numpy as jnp
        _gk = jax.random.key(seed)
        x = -0.0003929 + 0.9999 * jax.random.normal(jax.random.fold_in(_gk, 1), (8, 16, 16, 128), jnp.float32)
        return x
    x = _rec_inputs()

    def _L0_conv_setup():
        import jax, jax.numpy as jnp
        import numpy as np
        B, H, W, C = (8, 16, 16, 128)
        D = C // 8
        key = jax.random.key(seed)
        ks = jax.random.split(key, 5)
        scale = 1.0 / np.sqrt(C)
        return {'x': jax.random.normal(ks[0], (B, H, W, C), dtype=jnp.float32), 'Wf': jax.random.normal(ks[1], (C, D), dtype=jnp.float32) * scale, 'bf': jnp.zeros((D,), dtype=jnp.float32), 'Wg': jax.random.normal(ks[2], (C, D), dtype=jnp.float32) * scale, 'bg': jnp.zeros((D,), dtype=jnp.float32), 'Wh': jax.random.normal(ks[3], (C, D), dtype=jnp.float32) * scale, 'bh': jnp.zeros((D,), dtype=jnp.float32), 'Wv': jax.random.normal(ks[4], (D, C), dtype=jnp.float32) * (1.0 / np.sqrt(D)), 'bv': jnp.zeros((C,), dtype=jnp.float32), 'gamma': jnp.float32(0.01)}
    _L0_conv_all = _L0_conv_setup()
    _L0_conv_in = {k: v for k, v in _L0_conv_all.items() if k in ('Wf', 'bf', 'Wg', 'bg', 'Wh', 'bh', 'Wv', 'bv', 'gamma')}
    del _L0_conv_all

    def _L1_attn_setup():
        import jax, jax.numpy as jnp
        from jax import lax
        import numpy as np
        N_STEPS = 5
        key = jax.random.key(seed)
        kH, kv, k1, k2, k3 = jax.random.split(key, 5)
        B, S, D = (32, 128, 128)
        scale = 1.0 / np.sqrt(D)
        return {'H': jax.random.normal(kH, (B, S, D), dtype=jnp.float32), 'v': jax.random.normal(kv, (D, 1), dtype=jnp.float32) * scale, 'W1': jax.random.normal(k1, (D, D), dtype=jnp.float32) * scale, 'W2': jax.random.normal(k2, (D, D), dtype=jnp.float32) * scale, 'W3': jax.random.normal(k3, (D, D), dtype=jnp.float32) * scale}
    _L1_attn_all = _L1_attn_setup()
    _L1_attn_in = {k: v for k, v in _L1_attn_all.items() if k in ('v', 'W1', 'W2', 'W3')}
    del _L1_attn_all

    def _L1_ffn_setup():
        import jax, jax.numpy as jnp
        import numpy as np
        B, S, D, H, E = (4, 512, 128, 256, 8)
        key = jax.random.key(seed)
        ks = jax.random.split(key, 4)
        x = jax.random.normal(ks[0], (B, S, D), jnp.float32)
        Wr = jax.random.normal(ks[1], (E, D), jnp.float32) * 0.02
        br = jnp.zeros((E,), jnp.float32)
        W1 = jax.random.normal(ks[2], (E, D, H), jnp.float32) * 0.02
        b1 = jnp.zeros((E, H), jnp.float32)
        W2 = jax.random.normal(ks[3], (E, H, D), jnp.float32) * 0.02
        b2 = jnp.zeros((E, D), jnp.float32)
        return {'x': x, 'Wr': Wr, 'br': br, 'W1': W1, 'b1': b1, 'W2': W2, 'b2': b2}
    _L1_ffn_all = _L1_ffn_setup()
    _L1_ffn_in = {k: v for k, v in _L1_ffn_all.items() if k in ('Wr', 'br', 'W1', 'b1', 'W2', 'b2')}
    del _L1_ffn_all
    return {'x': x, 'L0_conv_Wf': _L0_conv_in['Wf'], 'L0_conv_bf': _L0_conv_in['bf'], 'L0_conv_Wg': _L0_conv_in['Wg'], 'L0_conv_bg': _L0_conv_in['bg'], 'L0_conv_Wh': _L0_conv_in['Wh'], 'L0_conv_bh': _L0_conv_in['bh'], 'L0_conv_Wv': _L0_conv_in['Wv'], 'L0_conv_bv': _L0_conv_in['bv'], 'L0_conv_gamma': _L0_conv_in['gamma'], 'L1_attn_v': _L1_attn_in['v'], 'L1_attn_W1': _L1_attn_in['W1'], 'L1_attn_W2': _L1_attn_in['W2'], 'L1_attn_W3': _L1_attn_in['W3'], 'L1_ffn_Wr': _L1_ffn_in['Wr'], 'L1_ffn_br': _L1_ffn_in['br'], 'L1_ffn_W1': _L1_ffn_in['W1'], 'L1_ffn_b1': _L1_ffn_in['b1'], 'L1_ffn_W2': _L1_ffn_in['W2'], 'L1_ffn_b2': _L1_ffn_in['b2']}

def reference(x, L0_conv_Wf, L0_conv_bf, L0_conv_Wg, L0_conv_bg, L0_conv_Wh, L0_conv_bh, L0_conv_Wv, L0_conv_bv, L0_conv_gamma, L1_attn_v, L1_attn_W1, L1_attn_W2, L1_attn_W3, L1_ffn_Wr, L1_ffn_br, L1_ffn_W1, L1_ffn_b1, L1_ffn_W2, L1_ffn_b2):
    import jax
    import jax.numpy as jnp

    def _L0_conv_ref(x, Wf, bf, Wg, bg, Wh, bh, Wv, bv, gamma):
        import jax, jax.numpy as jnp
        import numpy as np
        B, H, W, C = (8, 16, 16, 128)
        D = C // 8
        b, h, w, c = x.shape
        n = h * w
        xf = x.reshape(b, n, c)
        f = xf @ Wf + bf
        g = xf @ Wg + bg
        hh = xf @ Wh + bh
        s = jnp.einsum('bnd,bmd->bnm', f, g)
        attn = jax.nn.softmax(s, axis=-1)
        context = jnp.einsum('bnm,bmd->bnd', attn, hh)
        o = gamma * context @ Wv + bv + xf
        return o.reshape(b, h, w, c)

    def _L1_attn_ref(H, v, W1, W2, W3):
        import jax, jax.numpy as jnp
        from jax import lax
        import numpy as np
        N_STEPS = 5
        B, S, D = H.shape

        def step(carry, ht):
            H_prev, H_prev_tilde = carry
            temp = jnp.tanh(H_prev @ W1 + (ht @ W2)[:, None, :] + H_prev_tilde @ W3)
            w_t = jax.nn.softmax(temp @ v, axis=1)
            ht_hat = jnp.sum(H_prev_tilde * w_t, axis=1)
            ht_tilde = ht + jax.nn.relu(ht_hat)
            H_prev = jnp.concatenate([H_prev[:, 1:, :], ht[:, None, :]], axis=1)
            H_prev_tilde = jnp.concatenate([H_prev_tilde[:, 1:, :], ht_tilde[:, None, :]], axis=1)
            return ((H_prev, H_prev_tilde), ht_tilde)
        init = (jnp.zeros((B, N_STEPS, D), H.dtype), jnp.zeros((B, N_STEPS, D), H.dtype))
        _, ys = lax.scan(step, init, jnp.swapaxes(H, 0, 1))
        return jnp.swapaxes(ys, 0, 1)

    def _L1_ffn_ref(x, Wr, br, W1, b1, W2, b2):
        import jax, jax.numpy as jnp
        import numpy as np
        B, S, D, H, E = (4, 512, 128, 256, 8)
        b, s, d = x.shape
        n = b * s
        e = Wr.shape[0]
        xf = x.reshape(n, d)
        logits = xf @ Wr.T + br
        probs = jax.nn.softmax(logits, axis=-1)
        top2_prob, top2_idx = jax.lax.top_k(probs, 2)
        comb = jnp.zeros((n, e), x.dtype).at[jnp.arange(n)[:, None], top2_idx].add(top2_prob)
        h = jax.nn.gelu(jnp.einsum('nd,edh->enh', xf, W1) + b1[:, None, :], approximate=False)
        o = jnp.einsum('enh,ehd->end', h, W2) + b2[:, None, :]
        y = jnp.einsum('ne,end->nd', comb, o)
        return y.reshape(b, s, d)

    def _gn(v, G=32, eps=1e-05):
        B_, H_, W_, C_ = v.shape
        g = v.reshape(B_, H_, W_, G, C_ // G)
        m = jnp.mean(g, axis=(1, 2, 4), keepdims=True)
        s = jnp.var(g, axis=(1, 2, 4), keepdims=True)
        return ((g - m) / jnp.sqrt(s + eps)).reshape(v.shape)

    def _ln_c(v, eps=1e-06):
        m = jnp.mean(v, axis=-1, keepdims=True)
        s = jnp.var(v, axis=-1, keepdims=True)
        return (v - m) / jnp.sqrt(s + eps)

    def _ln_t(v, eps=1e-05):
        m = jnp.mean(v, axis=-1, keepdims=True)
        s = jnp.var(v, axis=-1, keepdims=True)
        return (v - m) / jnp.sqrt(s + eps)

    def _to_tokens(v):
        B_, H_, W_, C_ = v.shape
        return v.reshape(B_, H_ * W_, C_)

    def _from_tokens(t, like):
        return t.reshape(like.shape)
    x = _L0_conv_ref(x, L0_conv_Wf, L0_conv_bf, L0_conv_Wg, L0_conv_bg, L0_conv_Wh, L0_conv_bh, L0_conv_Wv, L0_conv_bv, L0_conv_gamma)
    t = _to_tokens(x)
    t = t + _L1_attn_ref(_ln_t(t), L1_attn_v, L1_attn_W1, L1_attn_W2, L1_attn_W3)
    t = t + _L1_ffn_ref(_ln_t(t), L1_ffn_Wr, L1_ffn_br, L1_ffn_W1, L1_ffn_b1, L1_ffn_W2, L1_ffn_b2)
    x = _from_tokens(t, x)
    return x

_drawn_inputs = setup_inputs


def setup_inputs(seed=0):
    import zlib

    import numpy as np

    out = dict(_drawn_inputs(seed))
    spreads = {'L0_conv_bf': (0.0, 0.8),
     'L0_conv_bg': (0.0, 0.8),
     'L0_conv_bh': (0.0, 0.8),
     'L0_conv_bv': (0.0, 0.1),
     'L1_ffn_br': (0.0, 0.8),
     'L1_ffn_b1': (0.0, 0.8),
     'L1_ffn_b2': (0.0, 0.8)}
    factors = {'L0_conv_Wf': 8.0,
     'L0_conv_Wg': 8.0,
     'L0_conv_Wh': 8.0,
     'L0_conv_Wv': 6.057,
     'L1_ffn_Wr': 8.0,
     'L1_ffn_W1': 8.0,
     'L1_ffn_W2': 8.0}
    for name, (base, spread) in spreads.items():
        noise = np.random.default_rng([zlib.crc32(name.encode()), seed]).standard_normal(out[name].shape)
        drawn = base * np.exp(spread * noise) if base else spread * noise
        out[name] = jnp.asarray(drawn.astype(out[name].dtype))
    for name, factor in factors.items():
        out[name] = (out[name] * factor).astype(out[name].dtype)
    return out
```

```python
from contextlib import ExitStack

import numpy as np

import concourse.bass as bass
from concourse import mybir

F32 = mybir.dt.float32
I32 = mybir.dt.int32
U32 = mybir.dt.uint32
ALU = mybir.AluOpType
ACT = mybir.ActivationFunctionType
AX_X = mybir.AxisListType.X

P = 128
B = 8
S = 256
D = 128
DH = 16
WIN = 5
OLD = WIN - 1
HALF = S // P
TS = 16
TILES = S // TS
E = 8
HID = 256
HH = HID // P
UNITS = E * HH
LEAD = 5
ACC_LAG = 9
W5 = WIN * B
W4 = OLD * B
HCOLS = (S + WIN) * B
STG = (TS + WIN) * B
EPS = 1e-5

NODES = 64
NODE_H = (np.log(22.0) - np.log(1e-8)) / (NODES - 1)


def node_constants():
    a = np.exp(np.log(1e-8) + NODE_H * np.arange(NODES)).astype(np.float32)
    h = np.float32(NODE_H)
    return a, h, float(np.sum(float(h) * np.tanh(a.astype(np.float64))))


def shape_constants():
    a, h, _ = node_constants()
    c = np.zeros((P, 2 * P + 1 + E + W4), np.float32)
    c[:, 0:P] = np.eye(P)
    c[0:NODES, P:2 * P] = h
    c[NODES, P:2 * P] = 1.0
    c[0:NODES, 2 * P] = a / 2
    c[:, 2 * P + 1:2 * P + 1 + E] = np.arange(E)
    for j in range(OLD):
        c[:, 2 * P + 1 + E + j * B:2 * P + 1 + E + (j + 1) * B] = -np.log(OLD - j)
    return c


def build(nc, x, Wf, bf, Wg, bg, Wh, bh, Wv, bv, gamma, v, W1, W2, W3, Wr, br, F1, b1, F2, b2, consts, out):
    K0 = node_constants()[2]
    x_tok_dram = x.rearrange("b h w c -> b (h w) c").rearrange("b (u p) c -> p (b u) c", p=P)
    out_dram = out.rearrange("b h w c -> b (h w) c")

    with ExitStack() as ctx:
        def sb(name, shape, dt=F32):
            return ctx.enter_context(nc.sbuf_tensor(name, shape, dt))

        def pair(name, shape, dt=F32):
            return [sb(f"{name}{i}", shape, dt) for i in range(2)]

        def sem(name):
            return ctx.enter_context(nc.semaphore(name))

        bank = [ctx.enter_context(nc.psum_tensor(f"bank{i}", [P, 512], F32)) for i in range(8)]

        cst = sb("cst", [P, 2 * P + 1 + E + W4])
        ident = cst[:, 0:P]
        fold_w = cst[:, P:2 * P]
        half_nodes = cst[0:NODES, 2 * P:2 * P + 1]
        iota8 = cst[:, 2 * P + 1:2 * P + 1 + E]
        g_init = cst[:, 2 * P + 1 + E:]
        w1 = sb("w1", [P, D])
        w2 = sb("w2", [P, D])
        w3 = sb("w3", [P, D])
        w3h = sb("w3h", [P, D])
        vcol = sb("vcol", [P, 1])
        vrep = sb("vrep", [P, P])
        nvrep = sb("nvrep", [P, P])
        wfg = sb("wfg", [P, 48])
        wh = sb("wh", [P, DH])
        bfg = sb("bfg", [48, 1])
        bhc = sb("bhc", [DH, 1])
        gam = sb("gam", [DH, 1])
        wv = sb("wv", [DH, P])
        bvc = sb("bvc", [P, 1])
        wr_rows = sb("wr_rows", [E, D])
        wrT = sb("wrT", [P, E])
        brb = sb("brb", [P, E])
        f1 = sb("f1", [P, E, HID])
        f2 = sb("f2", [P, UNITS, D])
        b1_rows = sb("b1_rows", [UNITS, P])
        b1T = sb("b1T", [P, UNITS])
        b2s = sb("b2s", [E, D])
        neghalf = sb("neghalf", [P, HALF])

        x_tok = sb("x_tok", [P, B * HALF, D])
        xT = sb("xT", [P, B, S])
        fT = sb("fT", [DH, B, S])
        gT = sb("gT", [DH, B, S])
        hh = sb("hh", [P, B * HALF, DH])
        nmax = pair("nmax", [P, HALF])
        esum = pair("esum", [P, HALF])
        rsum = pair("rsum", [P, HALF])
        prob = pair("prob", [P, HALF, S])
        probT = pair("probT", [P, HALF, S])
        ctxT = pair("ctxT", [DH, S])
        t1T = sb("t1T", [P, S, B])
        bst = pair("bst", [P, HALF, 6])
        bmv = pair("bmv", [P, HALF, 2])
        bve = pair("bve", [P, HALF])
        brs = pair("brs", [P, HALF])
        bnm = pair("bnm", [P, HALF])
        hn = pair("hn", [P, HALF, D])
        hT = sb("hT", [P, S + WIN, B])

        hst = pair("hst", [P, STG])
        T = pair("T", [P, W5])
        th = pair("th", [P, W5])
        GF = pair("GF", [P, W4])
        Z = pair("Z", [NODES, W4])
        Dy = pair("Dy", [P, W5])
        X = pair("X", [P, W5])
        Cm = pair("Cm", [P, W5])
        Q = pair("Q", [P, B])
        hM = pair("hM", [P, B])
        ybuf = pair("ybuf", [P, TS, B])

        t2T = sb("t2T", [P, B, TS])
        acc = pair("acc", [P, D])
        mst = sb("mst", [P, 6])
        mmv = sb("mmv", [P, 2])
        mve = sb("mve", [P, 1])
        mrs = sb("mrs", [P, 1])
        xn = sb("xn", [P, D])
        xnT = pair("xnT", [P, P])
        lg = sb("lg", [P, E])
        top = sb("top", [P, 8])
        topi = sb("topi", [P, 8], U32)
        topf = sb("topf", [P, 8])
        mask0 = sb("mask0", [P, E])
        mask = sb("mask", [P, E])
        dl = sb("dl", [P, E])
        ul = sb("ul", [P, E])
        rl = sb("rl", [P, E])
        r2 = sb("r2", [P, E])
        el = sb("el", [P, E])
        es = sb("es", [P, 1])
        ers = sb("ers", [P, 1])
        comb = pair("comb", [P, E])
        combT = sb("combT", [E, P])
        hid = pair("hid", [P, P])

        psA = bank[0:2]
        psS = bank[2:4]
        psH = bank[4]
        psO = bank[5:7]
        psT = bank[7]

        ld_cst, ld_x, ld_w, ld_attn, ld_ffn = (sem(n) for n in ("ld_cst", "ld_x", "ld_w", "ld_attn", "ld_ffn"))
        prep = sem("prep")
        pads, init = sem("pads"), sem("init")
        xt_ps, xt_sb, xt_sb_act, fg_ps, fg_sb, hh_ps, hh_sb = (sem(n) for n in ("xt_ps", "xt_sb", "xt_sb_act", "fg_ps", "fg_sb", "hh_ps", "hh_sb"))
        wt_ps, wt_sb = sem("wt_ps"), sem("wt_sb")
        sc_ps, mx_done, exp_done, rs_done, pn_done = (sem(n) for n in ("sc_ps", "mx_done", "exp_done", "rs_done", "pn_done"))
        pt_ps, pt_sb, cx_ps, cx_sb, o_ps, t1_done = (sem(n) for n in ("pt_ps", "pt_sb", "cx_ps", "cx_sb", "o_ps", "t1_done"))
        tk_ps, bst_done, bmv_done, bve_done, brs_done, bnm_done = (
            sem(n) for n in ("tk_ps", "bst_done", "bmv_done", "bve_done", "brs_done", "bnm_done"))
        hn_done, ht_ps, ht_done = sem("hn_done"), sem("ht_ps"), sem("ht_done")

        hst_loaded = sem("hst_loaded")
        projected = sem("projected")
        temp_ready = sem("temp_ready")
        score_ready = sem("score_ready")
        th_ready = sem("th_ready")
        x8_ready = sem("x8_ready")
        z_ready = sem("z_ready")
        q_ready = sem("q_ready")
        g_ready = sem("g_ready")
        f_ready = sem("f_ready")
        x_ready = sem("x_ready")
        y_ready = sem("y_ready")
        c_ready = sem("c_ready")
        dy_ready = sem("dy_ready")
        hm_ready = sem("hm_ready")

        t2_done, tok_ps, copied, stats, aggr, ve_done, rstd_done, xn_done, xn_ps, xnT_done, lg_ps = (
            sem(n) for n in ("t2_done", "tok_ps", "copied", "stats", "aggr", "ve_done", "rstd_done", "xn_done",
                             "xn_ps", "xnT_done", "lg_ps"))
        lg_done, top_done, topi_done, topf_done, m0_done, mask_done, dl_done, ul_done, rl_done, r2_done, el_done = (
            sem(n) for n in ("lg_done", "top_done", "topi_done", "topf_done", "m0_done", "mask_done", "dl_done",
                             "ul_done", "rl_done", "r2_done", "el_done"))
        es_done, ers_done, comb_done, ct_ps, ct_done, b2_ps, b2_done = (
            sem(n) for n in ("es_done", "ers_done", "comb_done", "ct_ps", "ct_done", "b2_ps", "b2_done"))
        up_ps, gelu_done = sem("up_ps"), sem("gelu_done")
        down_ps, acc_done = sem("down_ps"), sem("acc_done")
        stored = sem("stored")

        N_ATTN, N_FFN = 7, 5
        block = ctx.enter_context(nc.Block())

        def bc(ap, n=WIN):
            return ap.unsqueeze(1).to_broadcast([P, n, B])

        def in5(ap):
            return ap.rearrange("p (w b) -> p w b", b=B)

        def over_tiles(eng, tile):
            for k in range(2):
                tile(k, TS * k, TS, True)
            with eng.Fori(0, (TILES - 2) // 2) as p:
                base = p * (2 * TS)
                tile(2, base + 2 * TS, TS, True)
                tile(3, base + 3 * TS, TS, True)
            tile(TILES, TS * TILES, TS, False)
            tile(TILES + 1, TS * (TILES + 1), LEAD + ACC_LAG, False)

        def experts_step(k, base, i, last):
            j, jb = k - 1, base - TS
            j2, jb2 = k - 2, base - 2 * TS
            has, has2 = j >= 0 and not last, j2 >= 0
            unit = expert = None
            if i >= LEAD and has:
                unit = (j % 2, jb, i - LEAD)
            if i < LEAD and has2:
                unit = (j2 % 2, jb2, i - LEAD + UNITS)
            if i >= ACC_LAG and (i - ACC_LAG) % 2 == 0 and has:
                expert = (j % 2, jb, (i - ACC_LAG) // 2)
            if i < ACC_LAG and (i - ACC_LAG) % 2 == 0 and has2 and (i + TS - ACC_LAG) // 2 < E:
                expert = (j2 % 2, jb2, (i + TS - ACC_LAG) // 2)
            return ((j % 2, jb) if has else None), unit, expert

        @block.sync
        def _(sp):
            sp.dma_start(cst[:, :], consts).then_inc(ld_cst, 16)
            sp.dma_start(x_tok[:, :, :], x_tok_dram).then_inc(ld_x, 16)
            for dst, src in ((w1[:, :], W1), (w2[:, :], W2), (w3[:, :], W3), (vcol[:, :], v)):
                sp.dma_start(dst, src).then_inc(ld_w, 16)
            sp.dma_start(f1[:, :, :], F1.rearrange("e d h -> d e h")).then_inc(ld_ffn, 16)
            sp.dma_start(f2[:, :, :], F2.rearrange("e (u p) d -> p (e u) d", p=P)).then_inc(ld_ffn, 16)
            sp.wait_ge(ht_done, B)
            sp.wait_ge(pads, 1)
            for k in range(2):
                sp.dma_start(hst[k][:, :], hT[:, TS * k:TS * k + TS + WIN, :].rearrange("p t b -> p (t b)")
                             ).then_inc(hst_loaded, 16)
                sp.wait_ge(hst_loaded, 16 * (k + 1))

            def load(m, base):
                at = (base + TS) * B
                sp.wait_ge(th_ready, base + 1)
                flat = hT[:, :, :].rearrange("p t b -> p (t b)")
                sp.dma_start(hst[(m + 1) % 2][:, :], flat[:, bass.ds(at, STG)]
                             ).then_inc(hst_loaded, 16)

            def store(j, base):
                end = base + TS
                sp.wait_ge(acc_done, end)
                sp.wait_ge(b2_done, end)
                sp.dma_start(out_dram[:, bass.ds(base, TS), :], acc[j % 2][:, :]).then_inc(stored, 16)

            load(1, TS)
            with sp.Fori(0, (TILES - 4) // 2) as p:
                base = p * (2 * TS)
                for m in (2, 3):
                    load(m, base + m * TS)
                    store(m - 2, base + (m - 2) * TS)
            load(TILES - 2, (TILES - 2) * TS)
            for j in range(TILES - 4, TILES):
                store(j, j * TS)
            sp.wait_ge(stored, (TILES + 1) * TS)

        @block.gpsimd
        def _(pool):
            pool.memset(hT[:, S:S + WIN, :], 0.0).then_inc(pads, 1)
            pool.memset(neghalf[:, :], -0.5).then_inc(pads, 1)
            pool.memset(acc[1][:, :], 0.0).then_inc(stored, TS)
            pool.wait_ge(pads, 2)
            for b in range(B):
                pool.wait_ge(bve_done, b + 1)
                pool.tensor_tensor(brs[b % 2][:, :], bve[b % 2][:, :], neghalf[:, :], ALU.pow).then_inc(brs_done, 1)

            def tile(k, base, steps, chain):
                early, _, _ = experts_step(k, base, 0, k > TILES)
                if early:
                    jb = early[1]
                    pool.wait_ge(ve_done, jb + TS)
                    pool.tensor_tensor(mrs[:, :], mve[:, :], neghalf[:, 0:1], ALU.pow).then_inc(rstd_done, TS)

            over_tiles(pool, tile)

        @block.scalar
        def _(act):
            act.dma_start(wfg[:, 0:DH], Wf).then_inc(ld_attn, 16)
            act.dma_start(wfg[:, 32:32 + DH], Wg).then_inc(ld_attn, 16)
            act.dma_start(wh[:, :], Wh).then_inc(ld_attn, 16)
            act.dma_start(wv[:, :], Wv).then_inc(ld_attn, 16)
            act.dma_start(bfg[0:DH, :], bf.rearrange("(p o) -> p o", o=1)).then_inc(ld_attn, 16)
            act.dma_start(bfg[32:32 + DH, :], bg.rearrange("(p o) -> p o", o=1)).then_inc(ld_attn, 16)
            act.dma_start(bhc[:, :], bh.rearrange("(p o) -> p o", o=1)).then_inc(ld_attn, 16)
            act.dma_start(bvc[:, :], bv.rearrange("(p o) -> p o", o=1)).then_inc(ld_attn, 16)
            act.dma_start(gam[:, :], gamma.partition_broadcast(DH)).then_inc(ld_attn, 16)
            act.dma_start(brb[:, :], br.partition_broadcast(P)).then_inc(ld_ffn, 16)
            act.dma_start(wr_rows[:, :], Wr).then_inc(ld_ffn, 16)
            act.dma_start(b1_rows[:, :], b1.rearrange("e (u p) -> (e u) p", p=P)).then_inc(ld_ffn, 16)
            act.dma_start(b2s[:, :], b2).then_inc(ld_ffn, 16)

            for g in (1, 3):
                act.wait_ge(xt_ps, g + 1)
                act.copy(xT[:, 2 * g:2 * g + 2, :].rearrange("p b s -> p (b s)"), bank[g % 2][:, :]).then_inc(xt_sb_act, 1)
            act.wait_ge(hh_ps, 1)
            act.copy(hh[:, :, :].rearrange("p i d -> p (i d)"), bank[4][:, 0:B * HALF * DH]).then_inc(hh_sb, 1)

            def exp_rows(b):
                act.wait_ge(mx_done, b + 1)
                if b >= 2:
                    act.wait_ge(pt_ps, b - 1)
                for u in range(HALF):
                    act.activation(prob[b % 2][:, u, :], bank[b % 2][:, u * S:(u + 1) * S], ACT.Exp,
                                   bias=nmax[b % 2][:, u:u + 1], accum_out=esum[b % 2][:, u:u + 1]).then_inc(exp_done, 1)

            def copy_probT(b):
                act.wait_ge(pt_ps, b + 1)
                if b >= 2:
                    act.wait_ge(cx_ps, b - 1)
                act.copy(probT[b % 2][:, :, :].rearrange("p j n -> p (j n)"), bank[2 + b % 2][:, :]).then_inc(pt_sb, 1)

            def normalise(b):
                act.wait_ge(bnm_done, b + 1)
                act.wait_ge(brs_done, b + 1)
                if b >= 2:
                    act.wait_ge(ht_ps, b - 1)
                for u in range(HALF):
                    act.activation(hn[b % 2][:, u, :], bank[6][:, u * P:(u + 1) * P], ACT.Identity,
                                   bias=bnm[b % 2][:, u:u + 1], scale=brs[b % 2][:, u:u + 1]).then_inc(hn_done, 1)

            def copy_hT(b):
                act.wait_ge(ht_ps, b + 1)
                act.copy(hT[:, 0:S, b], bank[7][:, 0:S]).then_inc(ht_done, 1)

            for i in range(B + 3):
                if i < B:
                    exp_rows(i)
                if 0 <= i - 1 < B:
                    copy_probT(i - 1)
                if 0 <= i - 2 < B:
                    normalise(i - 2)
                if 0 <= i - 3 < B:
                    copy_hT(i - 3)

            act.wait_ge(prep, 1)
            act.activation(ul[:, :], vrep[:, 0:E], ACT.Gelu)
            act.wait_ge(projected, 1)
            act.activation(T[1][:, :], psA[1][:, 0:W5], ACT.Tanh).then_inc(temp_ready, 1)
            act.wait_ge(z_ready, 1)
            act.activation(GF[1][0:NODES, :], Z[1][:, :], ACT.Tanh, bias=half_nodes, scale=half_nodes).then_inc(f_ready, 1)

            def tile(k, base, steps, chain):
                for i in range(steps):
                    first = k == 0 and i == 0
                    n = base + i
                    p = (i - 1) % 2
                    early, unit, _ = experts_step(k, base, i, k > TILES)
                    if chain and not first:
                        act.wait_ge(projected, n + 1)
                        act.activation(T[p][:, :], psA[p][:, 0:W5], ACT.Tanh).then_inc(temp_ready, 1)
                    if early and i == 4:
                        act.wait_ge(xn_ps, early[1] + TS)
                        act.copy(xnT[early[0]][:, :], psT[:, 0:P]).then_inc(xnT_done, TS)
                    if early and i == 7:
                        act.wait_ge(dl_done, early[1] + TS)
                        act.activation(ul[:, :], dl[:, :], ACT.Tanh, scale=0.5).then_inc(ul_done, TS)
                    _, before, _ = (experts_step(k, base, i - 1, k > TILES) if i else
                                    experts_step(k - 1, base - TS, TS - 1, k - 1 > TILES))
                    if before:
                        jp, jb, u = before
                        act.wait_ge(up_ps, jb + u + 1)
                        act.activation(hid[u % 2][:, :], psH[:, 0:P], ACT.Gelu, bias=b1T[:, u:u + 1]
                                       ).then_inc(gelu_done, 1)
                    if chain and not first:
                        act.wait_ge(score_ready, n)
                        act.activation(th[p][:, 0:W4], psS[p][:, 0:W4], ACT.Tanh, bias=-K0 / 2, scale=0.5
                                       ).then_inc(th_ready, 1)
                        act.wait_ge(z_ready, n + 1)
                        act.activation(GF[p][0:NODES, :], Z[p][:, :], ACT.Tanh, bias=half_nodes, scale=half_nodes).then_inc(f_ready, 1)

            over_tiles(act, tile)

        @block.tensor
        def _(pe):
            pe.wait_ge(ld_cst, 16)
            pe.wait_ge(ld_x, 16)
            for g in range(4):
                if g >= 2:
                    pe.wait_ge((xt_sb, xt_sb_act)[g % 2], 1)
                for c in range(4):
                    mm = pe.transpose(bank[g % 2][:, c * P:(c + 1) * P], x_tok[:, 4 * g + c, :], ident)
                mm.then_inc(xt_ps, 1)
            pe.wait_ge(xt_sb, 2)
            pe.wait_ge(xt_sb_act, 2)
            pe.wait_ge(ld_attn, 16 * 9)
            pe.wait_ge(prep, 1)
            for c in range(4):
                if c >= 2:
                    pe.wait_ge(fg_sb, 2 * (c - 1))
                pe.matmul(bank[2 + c % 2][0:48, :], wfg[:, :], xT[:, 2 * c:2 * c + 2, :].rearrange("p b s -> p (b s)"),
                          start=True, stop=True).then_inc(fg_ps, 1)
            for t in range(B * HALF):
                mm = pe.matmul(bank[4][:, t * DH:(t + 1) * DH], xT[:, t // HALF, (t % HALF) * P:(t % HALF + 1) * P],
                               wh[:, :], start=True, stop=True)
            mm.then_inc(hh_ps, 1)
            pe.wait_ge(ld_ffn, 16 * 6)
            pe.transpose(bank[5][:, 0:E], wr_rows[:, :], ident[0:E, 0:E])
            pe.transpose(bank[5][:, 64:64 + UNITS], b1_rows[:, :], ident[0:UNITS, 0:UNITS]).then_inc(wt_ps, 1)
            pe.wait_ge(fg_sb, 8)

            def scores(b):
                if b >= 2:
                    pe.wait_ge(exp_done, 2 * (b - 1))
                for u in range(HALF):
                    mm = pe.matmul(bank[b % 2][:, u * S:(u + 1) * S], fT[:, b, u * P:(u + 1) * P], gT[:, b, :],
                                   start=True, stop=True)
                mm.then_inc(sc_ps, 1)

            def transpose_prob(b):
                pe.wait_ge(pn_done, b + 1)
                if b >= 2:
                    pe.wait_ge(pt_sb, b - 1)
                for j in range(HALF):
                    for u in range(HALF):
                        mm = pe.transpose(bank[2 + b % 2][:, j * S + u * P:j * S + (u + 1) * P],
                                          prob[b % 2][:, u, j * P:(j + 1) * P], ident)
                mm.then_inc(pt_ps, 1)

            def context(b):
                pe.wait_ge(pt_sb, b + 1)
                pe.wait_ge(hh_sb, 1)
                if b >= 1:
                    pe.wait_ge(cx_sb, b)
                for j in range(HALF):
                    mm = pe.matmul(bank[4][0:DH, 0:S], hh[:, HALF * b + j, :], probT[b % 2][:, j, :],
                                   start=(j == 0), stop=(j == HALF - 1))
                mm.then_inc(cx_ps, 1)

            def project_out(b):
                pe.wait_ge(cx_sb, b + 1)
                pe.wait_ge(wt_sb, 1)
                if b >= 1:
                    pe.wait_ge(t1_done, b)
                pe.matmul(bank[5][:, 0:S], wv[:, :], ctxT[b % 2][:, :], start=True, stop=True).then_inc(o_ps, 1)

            def transpose_t1(b):
                pe.wait_ge(t1_done, b + 1)
                if b >= 1:
                    pe.wait_ge(hn_done, 2 * b)
                    pe.wait_ge(bst_done, 2 * b)
                for u in range(HALF):
                    mm = pe.transpose(bank[6][:, u * P:(u + 1) * P], t1T[:, u * P:(u + 1) * P, b], ident)
                mm.then_inc(tk_ps, 1)

            def transpose_h(b):
                pe.wait_ge(hn_done, 2 * (b + 1))
                if b >= 1:
                    pe.wait_ge(ht_done, b)
                for u in range(HALF):
                    mm = pe.transpose(bank[7][:, u * P:(u + 1) * P], hn[b % 2][:, u, :], ident)
                mm.then_inc(ht_ps, 1)

            for i in range(B + 3):
                if i < B:
                    scores(i)
                if 0 <= i - 1 < B:
                    transpose_prob(i - 1)
                    context(i - 1)
                    project_out(i - 1)
                    transpose_t1(i - 1)
                if 0 <= i - 2 < B:
                    transpose_h(i - 2)

            pe.wait_ge(hst_loaded, 16)
            pe.wait_ge(exp_done, 2 * B)
            pe.wait_ge(ld_w, 16 * 4)
            pe.wait_ge(prep, 2)
            pe.matmul(psA[1][:, 0:W5], w2[:, :], hst[0][:, 0:W5], start=True, stop=True).then_inc(projected, 1)

            def item_sums(i, par, n):
                a, h = psA[i % 2][:, 0:W5], hst[par]
                pe.matmul(a, w2[:, :], h[:, (i + 1) * B:(i + 1 + WIN) * B], start=True, stop=False)
                pe.matmul(in5(a), w1[:, :], bc(h[:, i * B:(i + 1) * B]), start=False, stop=False)
                pe.wait_ge(hm_ready, n + 1)
                pe.matmul(in5(a), w3[:, :], bc(hM[i % 2][:, :]), start=False, stop=False)

            def early_work(i, par, jb):
                if i == 0:
                    pe.wait_ge(t2_done, jb + TS)
                    pe.transpose(psT[:, 0:P], t2T[:, :, :].rearrange("p b t -> p (b t)"), ident).then_inc(tok_ps, TS)
                if i == 3:
                    pe.wait_ge(xn_done, jb + TS)
                    pe.transpose(psT[:, 0:P], xn[:, :], ident).then_inc(xn_ps, TS)
                if i == 4:
                    pe.wait_ge(xnT_done, jb + TS)
                    pe.matmul(psT[:, 0:E], xnT[par][:, :], wrT[:, :], start=True, stop=True).then_inc(lg_ps, TS)
                if i == 10:
                    pe.wait_ge(comb_done, jb + TS)
                    pe.transpose(psT[0:E, 0:P], comb[par][:, :], ident).then_inc(ct_ps, TS)
                if i == 12:
                    pe.wait_ge(ct_done, jb + TS)
                    pe.matmul(psT[:, 0:P], combT[:, :], b2s[:, :], start=True, stop=True).then_inc(b2_ps, TS)

            def tile(k, base, steps, chain):
                for i in range(steps):
                    first = k == 0 and i == 0
                    n = base + i
                    p = (i - 1) % 2
                    early, unit, _ = experts_step(k, base, i, k > TILES)
                    if chain and not first:
                        pe.wait_ge(q_ready, n)
                        pe.matmul(in5(psA[p][:, 0:W5]), w3h[:, :], bc(Q[p][:, :]), start=False, stop=True
                                  ).then_inc(projected, 1)
                        if k == 0 and i == 1:
                            pe.wait_ge(temp_ready, 1)
                        pe.matmul(psS[p][:, 0:W4], nvrep[:, :], T[1 - p][:, B:W5], start=True, stop=False)
                        pe.wait_ge(f_ready, n)
                        pe.wait_ge(g_ready, n)
                        pe.matmul(psS[p][:, 0:W4], fold_w, GF[1 - p][:, :], start=False, stop=False)
                        pe.wait_ge(temp_ready, n + 1)
                        pe.matmul(psS[p][:, 0:W4], vrep[:, :], T[p][:, 0:W4], start=False, stop=True
                                  ).then_inc(score_ready, 1)
                    if chain:
                        if i == 0 and k > 0:
                            pe.wait_ge(hst_loaded, base + TS)
                        item_sums(i, k % 2, n)
                    if early:
                        early_work(i, *early)
                    _, before, _ = (experts_step(k, base, i - 1, k > TILES) if i else
                                    experts_step(k - 1, base - TS, TS - 1, k - 1 > TILES))
                    if before:
                        jp, jb, u = before
                        e, half = u // HH, u % HH
                        pe.wait_ge(gelu_done, jb + u + 1)
                        if half == 0 and not (k == 1 and e < 2):
                            pe.wait_ge(acc_done, jb + 2 * (e - 2) + 2)
                        mm = pe.matmul(psO[e % 2][:, 0:D], hid[u % 2][:, :], f2[:, u, :],
                                       start=(half == 0), stop=(half == HH - 1))
                        if half == HH - 1:
                            mm.then_inc(down_ps, 2)
                    if unit:
                        jp, jb, u = unit
                        if not before:
                            if not (k == 1 and u == 0):
                                pe.wait_ge(gelu_done, jb + u)
                        pe.matmul(psH[:, 0:P], f1[:, u // HH, (u % HH) * P:(u % HH + 1) * P], xnT[jp][:, :],
                                  start=True, stop=True).then_inc(up_ps, 1)

            over_tiles(pe, tile)

        @block.vector
        def _(dve):
            dve.memset(wfg[:, DH:32], 0.0)
            dve.wait_ge(ld_w, 16 * 4)
            dve.tensor_copy(vrep[:, :], vcol[:, 0:1].to_broadcast([P, P])).then_inc(prep, 1)
            dve.wait_ge(xt_ps, 1)
            dve.tensor_copy(xT[:, 0:2, :].rearrange("p b s -> p (b s)"), bank[0][:, :]).then_inc(xt_sb, 1)
            dve.wait_ge(xt_ps, 3)
            dve.tensor_copy(xT[:, 4:6, :].rearrange("p b s -> p (b s)"), bank[0][:, :]).then_inc(xt_sb, 1)
            dve.wait_ge(ld_attn, 16 * 9)
            for c in range(4):
                dve.wait_ge(fg_ps, c + 1)
                for dst, q in ((fT, 0), (gT, 32)):
                    dve.tensor_scalar(dst[:, 2 * c:2 * c + 2, :].rearrange("p b s -> p (b s)"),
                                      bank[2 + c % 2][q:q + DH, :], bfg[q:q + DH, 0:1], None, ALU.add
                                      ).then_inc(fg_sb, 1)
            dve.wait_ge(wt_ps, 1)
            dve.tensor_copy(wrT[:, :], bank[5][:, 0:E])
            dve.tensor_copy(b1T[:, :], bank[5][:, 64:64 + UNITS]).then_inc(wt_sb, 1)

            def row_max(b):
                dve.wait_ge(sc_ps, b + 1)
                if b >= 2:
                    dve.wait_ge(exp_done, 2 * (b - 1))
                dve.tensor_reduce(nmax[b % 2][:, :], bank[b % 2][:, :].rearrange("p (u m) -> p u m", u=HALF),
                                  AX_X, ALU.max, negate=True).then_inc(mx_done, 1)

            def normalise_prob(b):
                dve.wait_ge(exp_done, 2 * (b + 1))
                dve.reciprocal(rsum[b % 2][:, :], esum[b % 2][:, :]).then_inc(rs_done, 1)
                dve.wait_ge(rs_done, b + 1)
                for u in range(HALF):
                    ins = dve.tensor_scalar(prob[b % 2][:, u, :], prob[b % 2][:, u, :], rsum[b % 2][:, u:u + 1], None,
                                            ALU.mult)
                ins.then_inc(pn_done, 1)

            def context(b):
                dve.wait_ge(cx_ps, b + 1)
                if b >= 2:
                    dve.wait_ge(o_ps, b - 1)
                dve.tensor_scalar(ctxT[b % 2][:, :], bank[4][0:DH, 0:S], bhc[:, 0:1], gam[:, 0:1], ALU.add, ALU.mult
                                  ).then_inc(cx_sb, 1)

            def residual(b):
                dve.wait_ge(o_ps, b + 1)
                dve.scalar_tensor_tensor(t1T[:, :, b], bank[5][:, 0:S], bvc[:, 0:1], xT[:, b, :], ALU.add, ALU.add
                                         ).then_inc(t1_done, 1)

            def moments(b):
                dve.wait_ge(tk_ps, b + 1)
                for u in range(HALF):
                    dve.bn_stats(bst[b % 2][:, u, :], bank[6][:, u * P:(u + 1) * P]).then_inc(bst_done, 1)
                dve.wait_ge(bst_done, 2 * (b + 1))
                if b >= 2:
                    dve.wait_ge(bnm_done, b - 1)
                for u in range(HALF):
                    ins = dve.bn_aggr(bmv[b % 2][:, u, :], bst[b % 2][:, u, :])
                ins.then_inc(bmv_done, 1)
                dve.wait_ge(bmv_done, b + 1)
                if b >= 2:
                    dve.wait_ge(brs_done, b - 1)
                dve.tensor_scalar(bve[b % 2][:, :], bmv[b % 2][:, :, 1], EPS, None, ALU.add).then_inc(bve_done, 1)
                dve.wait_ge(brs_done, b + 1)
                if b >= 2:
                    dve.wait_ge(hn_done, 2 * (b - 1))
                dve.scalar_tensor_tensor(bnm[b % 2][:, :], bmv[b % 2][:, :, 0], -1.0, brs[b % 2][:, :], ALU.mult,
                                         ALU.mult).then_inc(bnm_done, 1)

            for i in range(B + 2):
                if i < B:
                    row_max(i)
                    normalise_prob(i)
                if 0 <= i - 1 < B:
                    context(i - 1)
                    residual(i - 1)
                    moments(i - 1)

            for q in range(2):
                dve.memset(th[q][:, W4:W5], 1.0).then_inc(init, 1)
                dve.memset(Cm[q][:, :], 0.0).then_inc(init, 1)
            dve.memset(Z[0][:, :], 1.0).then_inc(init, 1)
            dve.memset(GF[0][NODES:P, :], 0.0).then_inc(init, 1)
            dve.memset(Q[0][:, :], 0.0).then_inc(q_ready, 1)
            dve.tensor_scalar(nvrep[:, :], vrep[:, :], -1.0, None, ALU.mult)
            dve.wait_ge(ld_w, 16 * 4)
            dve.tensor_scalar(w3h[:, :], w3[:, :], 0.5, None, ALU.mult).then_inc(prep, 1)
            dve.tensor_copy(GF[1][NODES:P, :], g_init[NODES:P, :]).then_inc(g_ready, 1)
            dve.memset(Z[1][:, :], 1.0).then_inc(z_ready, 1)
            dve.wait_ge(init, 6)
            dve.wait_ge(hst_loaded, 16)
            h0 = hst[0][:, 0:B]
            dve.tensor_copy(hM[0][:, :], h0).then_inc(hm_ready, 1)
            dve.tensor_copy(ybuf[0][:, 0, :], h0).then_inc(y_ready, 1)
            dve.tensor_copy(in5(Dy[0][:, :]), bc(h0)).then_inc(dy_ready, 1)
            dve.tensor_copy(hM[1][:, :], hst[0][:, B:2 * B]).then_inc(hm_ready, 1)

            def early_work(i, par, jb):
                n = jb + TS
                if i == 0:
                    dve.wait_ge(y_ready, n)
                    t1 = t1T[:, :, :].rearrange("p t b -> p (t b)")[:, bass.ds(jb * B, TS * B)]
                    dve.tensor_tensor(t2T[:, :, :].rearrange("p b t -> p t b"), in5(t1), ybuf[par][:, :, :], ALU.add
                                      ).then_inc(t2_done, TS)
                if i == 1:
                    dve.wait_ge(tok_ps, n)
                    dve.bn_stats(mst[:, :], psT[:, 0:P]).then_inc(stats, TS)
                    if not isinstance(jb, int) or jb >= TS:
                        dve.wait_ge(stored, jb)
                    dve.tensor_copy(acc[par][:, :], psT[:, 0:P]).then_inc(copied, TS)
                if i == 2:
                    dve.wait_ge(stats, n)
                    dve.bn_aggr(mmv[:, :], mst[:, :]).then_inc(aggr, TS)
                    dve.wait_ge(aggr, n)
                    dve.tensor_scalar(mve[:, :], mmv[:, 1:2], EPS, None, ALU.add).then_inc(ve_done, TS)
                if i == 3:
                    dve.wait_ge(rstd_done, n)
                    dve.wait_ge(copied, n)
                    dve.tensor_scalar(xn[:, :], acc[par][:, :], mmv[:, 0:1], mrs[:, 0:1], ALU.subtract, ALU.mult
                                      ).then_inc(xn_done, TS)
                if i == 5:
                    dve.wait_ge(lg_ps, n)
                    dve.tensor_tensor(lg[:, :], psT[:, 0:E], brb[:, :], ALU.add).then_inc(lg_done, TS)
                    dve.wait_ge(lg_done, n)
                    dve.max(top[:, :], lg[:, :]).then_inc(top_done, TS)
                if i == 6:
                    dve.wait_ge(top_done, n)
                    dve.tensor_scalar(dl[:, :], lg[:, :], top[:, 0:1], None, ALU.subtract).then_inc(dl_done, TS)
                    dve.max_index(topi[:, :], top[:, :], lg[:, :]).then_inc(topi_done, TS)
                    dve.wait_ge(topi_done, n)
                    dve.tensor_copy(topf[:, :], topi[:, :]).then_inc(topf_done, TS)
                if i == 7:
                    dve.wait_ge(topf_done, n)
                    dve.tensor_scalar(mask0[:, :], iota8, topf[:, 0:1], None, ALU.is_equal).then_inc(m0_done, TS)
                    dve.wait_ge(m0_done, n)
                    dve.scalar_tensor_tensor(mask[:, :], iota8, topf[:, 1:2], mask0[:, :], ALU.is_equal, ALU.add
                                             ).then_inc(mask_done, TS)
                if i == 8:
                    dve.wait_ge(ul_done, n)
                    dve.tensor_scalar(rl[:, :], ul[:, :], -1.0, 1.0, ALU.mult, ALU.add).then_inc(rl_done, TS)
                    dve.wait_ge(rl_done, n)
                    dve.reciprocal(r2[:, :], rl[:, :]).then_inc(r2_done, TS)
                    dve.wait_ge(r2_done, n)
                    dve.tensor_scalar(el[:, :], r2[:, :], 2.0, -1.0, ALU.mult, ALU.add).then_inc(el_done, TS)
                if i == 9:
                    dve.wait_ge(el_done, n)
                    dve.reduce_sum(es[:, :], el[:, :], AX_X).then_inc(es_done, TS)
                    dve.wait_ge(es_done, n)
                    dve.reciprocal(ers[:, :], es[:, :]).then_inc(ers_done, TS)
                    dve.wait_ge(ers_done, n)
                    dve.wait_ge(mask_done, n)
                    dve.scalar_tensor_tensor(comb[par][:, :], el[:, :], ers[:, 0:1], mask[:, :], ALU.mult, ALU.mult
                                             ).then_inc(comb_done, TS)
                if i == 11:
                    dve.wait_ge(ct_ps, n)
                    dve.tensor_copy(combT[:, :], psT[0:E, 0:P]).then_inc(ct_done, TS)
                if i == 13:
                    dve.wait_ge(b2_ps, n)
                    dve.wait_ge(acc_done, jb + 2 * ((i - ACC_LAG) // 2))
                    dve.tensor_tensor(acc[par][:, :], acc[par][:, :], psT[:, 0:P], ALU.add).then_inc(b2_done, TS)

            def add_expert(par, jb, e):
                dve.wait_ge(down_ps, jb + 2 * (e + 1))
                if e == 0:
                    dve.wait_ge(comb_done, jb + TS)
                    dve.wait_ge(copied, jb + TS)
                else:
                    dve.wait_ge(acc_done, jb + 2 * e)
                if e == (13 - ACC_LAG) // 2:
                    dve.wait_ge(b2_done, jb + TS)
                dve.scalar_tensor_tensor(acc[par][:, :], psO[e % 2][:, 0:D], comb[par][:, e:e + 1], acc[par][:, :],
                                         ALU.mult, ALU.add).then_inc(acc_done, 2)

            def tile(k, base, steps, chain):
                for i in range(steps):
                    n = base + i
                    p, q = (i - 1) % 2, i % 2
                    early, _, expert = experts_step(k, base, i, k > TILES)
                    if chain and not (k == 0 and i == 0):
                        dve.wait_ge(th_ready, n)
                        dve.wait_ge(dy_ready, n)
                        dve.scalar_tensor_tensor(X[p][:, 0:B], th[p][:, 0:B], 1.0, Dy[p][:, 0:B], ALU.add, ALU.mult
                                                 ).then_inc(x8_ready, 1)
                        dve.scalar_tensor_tensor(Z[p][:, 0:W4 - B], th[p][0:NODES, B:W4], -1.0, th[p][0:NODES, B:W4],
                                                 ALU.mult, ALU.max).then_inc(z_ready, 1)
                        dve.wait_ge(x8_ready, n)
                        dve.tensor_tensor(Q[q][:, :], X[p][:, 0:B], Cm[p][:, 0:B], ALU.max).then_inc(q_ready, 1)
                        dve.tensor_scalar(GF[p][NODES:P, 0:W4 - B], psS[p][NODES:P, B:W4], -K0, 0.0, ALU.add, ALU.min
                                          ).then_inc(g_ready, 1)
                        dve.wait_ge(q_ready, n + 1)
                        dve.scalar_tensor_tensor(ybuf[k % 2][:, i, :], Q[q][:, :], 0.5, hM[q][:, :], ALU.mult, ALU.add
                                                 ).then_inc(y_ready, 1)
                        dve.scalar_tensor_tensor(X[p][:, B:W5], th[p][:, B:W5], 1.0, Dy[p][:, B:W5], ALU.add, ALU.mult
                                                 ).then_inc(x_ready, 1)
                        dve.wait_ge(x_ready, n)
                        dve.tensor_tensor(Cm[q][:, 0:W4], Cm[p][:, B:W5], X[p][:, B:W5], ALU.subtract
                                          ).then_inc(c_ready, 1)
                        dve.wait_ge(c_ready, n)
                        dve.wait_ge(y_ready, n + 1)
                        dve.scalar_tensor_tensor(in5(Dy[q][:, :]), in5(Cm[q][:, :]), 0.5, bc(ybuf[k % 2][:, i, :]),
                                                 ALU.mult, ALU.add).then_inc(dy_ready, 1)
                        if i == 0:
                            dve.wait_ge(hst_loaded, base + TS)
                        dve.scalar_tensor_tensor(hM[p][:, :], Cm[q][:, 0:B], -0.5, hst[k % 2][:, (i + 1) * B:(i + 2) * B],
                                                 ALU.mult, ALU.add).then_inc(hm_ready, 1)
                    if early:
                        early_work(i, *early)
                    if expert:
                        add_expert(*expert)

            over_tiles(dve, tile)


_INS = ["x", "L0_conv_Wf", "L0_conv_bf", "L0_conv_Wg", "L0_conv_bg", "L0_conv_Wh", "L0_conv_bh", "L0_conv_Wv",
        "L0_conv_bv", "L0_conv_gamma", "L1_attn_v", "L1_attn_W1", "L1_attn_W2", "L1_attn_W3", "L1_ffn_Wr",
        "L1_ffn_br", "L1_ffn_W1", "L1_ffn_b1", "L1_ffn_W2", "L1_ffn_b2"]


def kernel(**inputs):
    import numpy as _np
    import concourse.bacc as _bacc
    from concourse import mybir as _mybir
    from concourse.bass_utils import run_bass_kernel_spmd as _run

    nc = _bacc.Bacc("TRN2", target_bir_lowering=False, num_devices=1)
    arrays, args = {}, []
    for name in _INS:
        a = _np.ascontiguousarray(inputs[name])
        arrays[f"in_{name}_dram"] = a
        args.append(nc.dram_tensor(f"in_{name}_dram", a.shape, _mybir.dt.from_np(a.dtype), kind="ExternalInput").ap())
    c = shape_constants()
    arrays["shape_constants_dram"] = c
    args.append(nc.dram_tensor("shape_constants_dram", c.shape, F32, kind="ExternalInput").ap())
    args.append(nc.dram_tensor("out_0_dram", (8, 16, 16, 128), F32, kind="ExternalOutput").ap())
    build(nc, *args)
    r = _run(nc, [arrays], core_ids=[0])
    return r.results[0]["out_0_dram"]
```

```python
from contextlib import ExitStack

import numpy as np

import concourse.bass as bass
from concourse import mybir

F32 = mybir.dt.float32
BF16 = mybir.dt.bfloat16
F16 = mybir.dt.float16
I32 = mybir.dt.int32
U32 = mybir.dt.uint32
ALU = mybir.AluOpType
ACT = mybir.ActivationFunctionType
AX_X = mybir.AxisListType.X

P = 128
B = 8
S = 256
D = 128
DH = 16
WIN = 5
OLD = WIN - 1
HALF = S // P
TS = 16
TILES = S // TS
E = 8
HID = 256
HH = HID // P
UNITS = E * HH
LEAD = 7
ACC_LAG = 12
W5 = WIN * B
W4 = OLD * B
HCOLS = (S + WIN) * B
STG = (TS + WIN) * B
B2_STEP = 15
EPS = 1e-5
WS = 64.0

NODES = 64
NODE_H = (np.log(22.0) - np.log(1e-8)) / (NODES - 1)


def node_constants():
    a = np.exp(np.log(1e-8) + NODE_H * np.arange(NODES)).astype(np.float32)
    h = np.float32(NODE_H)
    return a, h, float(np.sum(float(h) * np.tanh(a.astype(np.float64))))


def shape_constants():
    a, h, _ = node_constants()
    c = np.zeros((P, 2 * P + 1 + E + W4), np.float32)
    c[:, 0:P] = np.eye(P)
    c[0:NODES, P:2 * P] = h * np.float32(WS)
    c[NODES, P:2 * P] = 1.0
    c[0:NODES, 2 * P] = a / 2
    c[:, 2 * P + 1:2 * P + 1 + E] = np.arange(E)
    for j in range(OLD):
        c[:, 2 * P + 1 + E + j * B:2 * P + 1 + E + (j + 1) * B] = -np.log(OLD - j) * WS
    return c


def build(nc, x, Wf, bf, Wg, bg, Wh, bh, Wv, bv, gamma, v, W1, W2, W3, Wr, br, F1, b1, F2, b2, consts, out):
    K0 = node_constants()[2]
    x_tok_dram = x.rearrange("b h w c -> b (h w) c").rearrange("b (u p) c -> p (b u) c", p=P)
    out_dram = out.rearrange("b h w c -> b (h w) c")

    with ExitStack() as ctx:
        def sb(name, shape, dt=F32):
            return ctx.enter_context(nc.sbuf_tensor(name, shape, dt))

        def pair(name, shape, dt=F32):
            return [sb(f"{name}{i}", shape, dt) for i in range(2)]

        def sem(name):
            return ctx.enter_context(nc.semaphore(name))

        bank = [ctx.enter_context(nc.psum_tensor(f"bank{i}", [P, 512], F32)) for i in range(8)]

        cst = sb("cst", [P, 2 * P + 1 + E + W4])
        ident = cst[:, 0:P]
        fold_w = cst[:, P:2 * P]
        half_nodes = cst[0:NODES, 2 * P:2 * P + 1]
        iota8 = cst[:, 2 * P + 1:2 * P + 1 + E]
        g_init = cst[:, 2 * P + 1 + E:]
        w1 = sb("w1", [P, D])
        w2 = sb("w2", [P, D])
        w3 = sb("w3", [P, D])
        w13 = sb("w13", [P, D])
        vcol = sb("vcol", [P, 1])
        vrep = sb("vrep", [P, P])
        def parts(name, n):
            return [sb(f"{name}_{i}", [P, n], F16) for i in range(2)]

        w2p, w3p, w13p, vp, nvp, wrp = (parts(n, P if n != "wrp" else E) for n in ("w2p", "w3p", "w13p", "vp", "nvp", "wrp"))
        f1p = parts("f1p", E * HID)
        f1s = sb("f1s", [P, E * HID])
        wfg = sb("wfg", [P, 48])
        wh = sb("wh", [P, DH])
        bfg = sb("bfg", [48, 1])
        bhc = sb("bhc", [DH, 1])
        gam = sb("gam", [DH, 1])
        wv = sb("wv", [DH, P])
        bvc = sb("bvc", [P, 1])
        wr_rows = sb("wr_rows", [E, D])
        wrT = sb("wrT", [P, E])
        brb = sb("brb", [P, E])
        f1 = sb("f1", [P, E, HID])
        f2 = sb("f2", [P, UNITS, D])
        b1_rows = sb("b1_rows", [UNITS, P])
        b1T = sb("b1T", [P, UNITS])
        b2s = sb("b2s", [E, D])
        neghalf = sb("neghalf", [P, HALF])

        x_tok = sb("x_tok", [P, B * HALF, D])
        xT = sb("xT", [P, B, S])
        fT = sb("fT", [DH, B, S])
        gT = sb("gT", [DH, B, S])
        hh = sb("hh", [P, B * HALF, DH])
        nmax = pair("nmax", [P, HALF])
        esum = pair("esum", [P, HALF])
        rsum = pair("rsum", [P, HALF])
        prob = pair("prob", [P, HALF, S])
        probT = pair("probT", [P, HALF, S])
        ctxT = pair("ctxT", [DH, S])
        t1T = sb("t1T", [P, S, B])
        bst = pair("bst", [P, HALF, 6])
        bmv = pair("bmv", [P, HALF, 2])
        bve = pair("bve", [P, HALF])
        brs = pair("brs", [P, HALF])
        bnm = pair("bnm", [P, HALF])
        hn = pair("hn", [P, HALF, D])
        hT = sb("hT", [P, S + WIN, B])
        hp = [sb(f"hp{i}", [P, S + WIN, B], F16) for i in range(2)]

        hst = pair("hst", [P, STG])
        hpst = [pair(f"hpst{i}_", [P, STG], F16) for i in range(2)]
        Tf = pair("Tf", [P, W5])
        Tp = [pair(f"Tp{i}_", [P, W5], F16) for i in range(2)]
        th = pair("th", [P, W5, 2])
        GF = pair("GF", [P, W4])
        Z = pair("Z", [NODES, W4])
        DE = pair("DE", [P, W5, 2])
        CC = pair("CC", [P, W5 + B, 2])
        Rp = [pair(f"Rp{i}_", [P, B], F16) for i in range(2)]
        yh = sb("yh", [P, B])
        ybuf = pair("ybuf", [P, TS, B])

        t2T = sb("t2T", [P, B, TS])
        acc = pair("acc", [P, D])
        mst = sb("mst", [P, 6])
        mmv = sb("mmv", [P, 2])
        mve = sb("mve", [P, 1])
        mrs = sb("mrs", [P, 1])
        xn = sb("xn", [P, D])
        xnT = [pair(f"xnT{i}_", [P, P], F16) for i in range(2)]
        lg = sb("lg", [P, E])
        top = sb("top", [P, 8])
        topi = sb("topi", [P, 8], U32)
        topf = sb("topf", [P, 8])
        mask0 = sb("mask0", [P, E])
        mask = sb("mask", [P, E])
        dl = sb("dl", [P, E])
        ul = sb("ul", [P, E])
        rl = sb("rl", [P, E])
        el = sb("el", [P, E])
        es = sb("es", [P, 1])
        ers = sb("ers", [P, 1])
        r2 = sb("r2", [P, E])
        comb = pair("comb", [P, E])
        combT = sb("combT", [E, P])
        hid = pair("hid", [P, P])

        psA = bank[0:2]
        psS = bank[2:4]
        psH = bank[4]
        psO = bank[5:7]
        psT = bank[7]

        ld_cst, ld_x, ld_w, ld_attn, ld_ffn = (sem(n) for n in ("ld_cst", "ld_x", "ld_w", "ld_attn", "ld_ffn"))
        prep = sem("prep")
        pads, init = sem("pads"), sem("init")
        xt_ps, xt_sb, xt_sb_act, fg_ps, fg_sb, hh_ps, hh_sb = (sem(n) for n in ("xt_ps", "xt_sb", "xt_sb_act", "fg_ps", "fg_sb", "hh_ps", "hh_sb"))
        wt_ps, wt_sb = sem("wt_ps"), sem("wt_sb")
        sc_ps, mx_done, exp_done, rs_done, pn_done = (sem(n) for n in ("sc_ps", "mx_done", "exp_done", "rs_done", "pn_done"))
        pt_ps, pt_sb, cx_ps, cx_sb, o_ps, t1_done = (sem(n) for n in ("pt_ps", "pt_sb", "cx_ps", "cx_sb", "o_ps", "t1_done"))
        tk_ps, bst_done, bmv_done, bve_done, brs_done, bnm_done = (
            sem(n) for n in ("tk_ps", "bst_done", "bmv_done", "bve_done", "brs_done", "bnm_done"))
        hn_done, ht_ps, ht_done = sem("hn_done"), sem("ht_ps"), sem("ht_done")

        hst_loaded = sem("hst_loaded")
        hpst_loaded = [sem(f"hpst_loaded{i}") for i in range(2)]
        h1_done, h2_done = sem("h1_done"), sem("h2_done")
        split, fsplit = sem("split"), sem("fsplit")
        projected = sem("projected")
        t1_ready = sem("t1_ready")
        tf_ready = sem("tf_ready")
        t2_ready = sem("t2_ready")
        score_ready = sem("score_ready")
        th_ready = sem("th_ready")
        crit_ready = sem("crit_ready")
        z_ready = sem("z_ready")
        r1_ready = sem("r1_ready")
        r2_ready = sem("r2_ready")
        g_ready = sem("g_ready")
        f_ready = sem("f_ready")
        y_ready = sem("y_ready")
        yh_ready = sem("yh_ready")
        c_ready = sem("c_ready")
        d_ready = sem("d_ready")
        e_ready = sem("e_ready")

        t2_done, tok_ps, copied, stats, aggr, ve_done, rstd_done, xn_done, xn_ps, xnT_done, xnT2_done, lg_ps = (
            sem(n) for n in ("t2_done", "tok_ps", "copied", "stats", "aggr", "ve_done", "rstd_done", "xn_done",
                             "xn_ps", "xnT_done", "xnT2_done", "lg_ps"))
        lg_done, top_done, topi_done, topf_done, m0_done, mask_done, dl_done, ul_done, rl_done, r2_done, el_done = (
            sem(n) for n in ("lg_done", "top_done", "topi_done", "topf_done", "m0_done", "mask_done", "dl_done",
                             "ul_done", "rl_done", "r2_done", "el_done"))
        es_done, ers_done, comb_done, ct_ps, ct_done, b2_ps, b2_done = (
            sem(n) for n in ("es_done", "ers_done", "comb_done", "ct_ps", "ct_done", "b2_ps", "b2_done"))
        up_ps, gelu_done = sem("up_ps"), sem("gelu_done")
        down_ps, acc_done = sem("down_ps"), sem("acc_done")
        stored = sem("stored")

        SPLITS = 4 * 2 + 2 + 2
        block = ctx.enter_context(nc.Block())

        def bc(ap, n=WIN):
            return ap.unsqueeze(1).to_broadcast([P, n, B])

        def in5(ap):
            return ap.rearrange("p (w b) -> p w b", b=B)

        def over_tiles(eng, tile):
            for k in range(2):
                tile(k, TS * k, TS, True)
            with eng.Fori(0, (TILES - 2) // 2) as p:
                base = p * (2 * TS)
                tile(2, base + 2 * TS, TS, True)
                tile(3, base + 3 * TS, TS, True)
            tile(TILES, TS * TILES, TS, False)
            tile(TILES + 1, TS * (TILES + 1), ACC_LAG, False)

        def experts_step(k, base, i, last):
            j, jb = k - 1, base - TS
            j2, jb2 = k - 2, base - 2 * TS
            has, has2 = j >= 0 and not last, j2 >= 0
            unit = expert = None
            if i >= LEAD and has:
                unit = (j % 2, jb, i - LEAD)
            if i < LEAD and has2:
                unit = (j2 % 2, jb2, i - LEAD + UNITS)
            if i >= ACC_LAG and (i - ACC_LAG) % 2 == 0 and has:
                expert = (j % 2, jb, (i - ACC_LAG) // 2)
            if i < ACC_LAG and (i - ACC_LAG) % 2 == 0 and has2 and (i + TS - ACC_LAG) // 2 < E:
                expert = (j2 % 2, jb2, (i + TS - ACC_LAG) // 2)
            return ((j % 2, jb) if has else None), unit, expert

        @block.sync
        def _(sp):
            sp.dma_start(cst[:, :], consts).then_inc(ld_cst, 16)
            sp.dma_start(x_tok[:, :, :], x_tok_dram).then_inc(ld_x, 16)
            for dst, src in ((w1[:, :], W1), (w2[:, :], W2), (w3[:, :], W3), (vcol[:, :], v)):
                sp.dma_start(dst, src).then_inc(ld_w, 16)
            sp.dma_start(f1[:, :, :], F1.rearrange("e d h -> d e h")).then_inc(ld_ffn, 16)
            sp.dma_start(f2[:, :, :], F2.rearrange("e (u p) d -> p (e u) d", p=P)).then_inc(ld_ffn, 16)
            sp.wait_ge(ht_done, B)
            sp.wait_ge(pads, 3)
            sp.wait_ge(h2_done, B)
            staged = [(hT, hst, hst_loaded)] + [(hp[i], hpst[i], hpst_loaded[i]) for i in range(2)]
            for k in range(2):
                for src, dst, done in staged:
                    if k:
                        sp.wait_ge(done, 16)
                    sp.dma_start(dst[k][:, :], src[:, TS * k:TS * k + TS + WIN, :].rearrange("p t b -> p (t b)")
                                 ).then_inc(done, 16)

            def load(m, base):
                at = (base + TS) * B
                sp.wait_ge(th_ready, base + 1)
                for src, dst, done in staged:
                    flat = src[:, :, :].rearrange("p t b -> p (t b)")
                    sp.dma_start(dst[(m + 1) % 2][:, :], flat[:, bass.ds(at, STG)]).then_inc(done, 16)

            def store(j, base):
                end = base + TS
                sp.wait_ge(acc_done, end)
                sp.wait_ge(b2_done, end)
                sp.dma_start(out_dram[:, bass.ds(base, TS), :], acc[j % 2][:, :]).then_inc(stored, 16)

            load(1, TS)
            with sp.Fori(0, (TILES - 4) // 2) as p:
                base = p * (2 * TS)
                for m in (2, 3):
                    load(m, base + m * TS)
                    store(m - 2, base + (m - 2) * TS)
            load(TILES - 2, (TILES - 2) * TS)
            for j in range(TILES - 4, TILES):
                store(j, j * TS)
            sp.wait_ge(stored, (TILES + 1) * TS)

        @block.gpsimd
        def _(pool):
            for t in [hT] + hp:
                pool.memset(t[:, S:S + WIN, :], 0.0).then_inc(pads, 1)
            pool.memset(neghalf[:, :], -0.5).then_inc(pads, 1)
            pool.memset(acc[1][:, :], 0.0).then_inc(stored, TS)
            pool.wait_ge(pads, 4)
            for b in range(B):
                pool.wait_ge(bve_done, b + 1)
                pool.tensor_tensor(brs[b % 2][:, :], bve[b % 2][:, :], neghalf[:, :], ALU.pow).then_inc(brs_done, 1)

            pool.tensor_scalar(f1s[:, :], f1[:, :, :].rearrange("p e h -> p (e h)"), WS, None, ALU.mult).then_inc(fsplit, 1)
            pool.wait_ge(fsplit, 1)
            pool.tensor_copy(f1p[0][:, :], f1s[:, :]).then_inc(fsplit, 1)
            pool.wait_ge(fsplit, 2)
            pool.tensor_tensor(f1p[1][:, :], f1s[:, :], f1p[0][:, :], ALU.subtract).then_inc(fsplit, 1)

            def tile(k, base, steps, chain):
                early, _, _ = experts_step(k, base, 0, k > TILES)
                if early:
                    jb = early[1]
                    pool.wait_ge(ve_done, jb + TS)
                    pool.tensor_tensor(mrs[:, :], mve[:, :], neghalf[:, 0:1], ALU.pow).then_inc(rstd_done, TS)

            over_tiles(pool, tile)

        @block.scalar
        def _(act):
            act.dma_start(wfg[:, 0:DH], Wf).then_inc(ld_attn, 16)
            act.dma_start(wfg[:, 32:32 + DH], Wg).then_inc(ld_attn, 16)
            act.dma_start(wh[:, :], Wh).then_inc(ld_attn, 16)
            act.dma_start(wv[:, :], Wv).then_inc(ld_attn, 16)
            act.dma_start(bfg[0:DH, :], bf.rearrange("(p o) -> p o", o=1)).then_inc(ld_attn, 16)
            act.dma_start(bfg[32:32 + DH, :], bg.rearrange("(p o) -> p o", o=1)).then_inc(ld_attn, 16)
            act.dma_start(bhc[:, :], bh.rearrange("(p o) -> p o", o=1)).then_inc(ld_attn, 16)
            act.dma_start(bvc[:, :], bv.rearrange("(p o) -> p o", o=1)).then_inc(ld_attn, 16)
            act.dma_start(gam[:, :], gamma.partition_broadcast(DH)).then_inc(ld_attn, 16)
            act.dma_start(brb[:, :], br.partition_broadcast(P)).then_inc(ld_ffn, 16)
            act.dma_start(wr_rows[:, :], Wr).then_inc(ld_ffn, 16)
            act.dma_start(b1_rows[:, :], b1.rearrange("e (u p) -> (e u) p", p=P)).then_inc(ld_ffn, 16)
            act.dma_start(b2s[:, :], b2).then_inc(ld_ffn, 16)

            for g in (1, 3):
                act.wait_ge(xt_ps, g + 1)
                act.copy(xT[:, 2 * g:2 * g + 2, :].rearrange("p b s -> p (b s)"), bank[g % 2][:, :]).then_inc(xt_sb_act, 1)
            act.wait_ge(hh_ps, 1)
            act.copy(hh[:, :, :].rearrange("p i d -> p (i d)"), bank[4][:, 0:B * HALF * DH]).then_inc(hh_sb, 1)

            def exp_rows(b):
                act.wait_ge(mx_done, b + 1)
                if b >= 2:
                    act.wait_ge(pt_ps, b - 1)
                for u in range(HALF):
                    act.activation(prob[b % 2][:, u, :], bank[b % 2][:, u * S:(u + 1) * S], ACT.Exp,
                                   bias=nmax[b % 2][:, u:u + 1], accum_out=esum[b % 2][:, u:u + 1]).then_inc(exp_done, 1)

            def copy_probT(b):
                act.wait_ge(pt_ps, b + 1)
                if b >= 2:
                    act.wait_ge(cx_ps, b - 1)
                act.copy(probT[b % 2][:, :, :].rearrange("p j n -> p (j n)"), bank[2 + b % 2][:, :]).then_inc(pt_sb, 1)

            def normalise(b):
                act.wait_ge(bnm_done, b + 1)
                act.wait_ge(brs_done, b + 1)
                if b >= 2:
                    act.wait_ge(ht_ps, b - 1)
                for u in range(HALF):
                    act.activation(hn[b % 2][:, u, :], bank[6][:, u * P:(u + 1) * P], ACT.Identity,
                                   bias=bnm[b % 2][:, u:u + 1], scale=brs[b % 2][:, u:u + 1]).then_inc(hn_done, 1)

            def copy_hT(b):
                act.wait_ge(ht_ps, b + 1)
                act.copy(hp[0][:, 0:S, b], bank[7][:, 0:S]).then_inc(h1_done, 1)
                act.copy(hT[:, 0:S, b], bank[7][:, 0:S]).then_inc(ht_done, 1)

            for i in range(B + 3):
                if 0 <= i - 1 < B:
                    copy_probT(i - 1)
                if i < B:
                    exp_rows(i)
                if 0 <= i - 2 < B:
                    normalise(i - 2)
                if 0 <= i - 3 < B:
                    copy_hT(i - 3)

            def tanh_of_item(p):
                act.activation(Tp[0][p][:, :], psA[p][:, 0:W5], ACT.Tanh, scale=1 / WS).then_inc(t1_ready, 1)
                act.activation(Tf[p][:, :], psA[p][:, 0:W5], ACT.Tanh, scale=1 / WS).then_inc(tf_ready, 1)

            act.wait_ge(prep, 1)
            act.activation(ul[:, :], vrep[:, 0:E], ACT.Gelu)
            act.wait_ge(projected, 1)
            tanh_of_item(1)
            act.wait_ge(z_ready, 1)
            act.activation(GF[1][0:NODES, :], Z[1][:, :], ACT.Tanh, bias=half_nodes, scale=half_nodes).then_inc(f_ready, 1)

            def tile(k, base, steps, chain):
                for i in range(steps):
                    first = k == 0 and i == 0
                    n = base + i
                    p = (i - 1) % 2
                    early, unit, _ = experts_step(k, base, i, k > TILES)
                    if chain and not first:
                        act.wait_ge(projected, n + 1)
                        tanh_of_item(p)
                    _, before, _ = (experts_step(k, base, i - 1, k > TILES) if i else
                                    experts_step(k - 1, base - TS, TS - 1, k - 1 > TILES))
                    if before:
                        jp, jb, u = before
                        act.wait_ge(up_ps, jb + u + 1)
                        act.activation(hid[u % 2][:, :], psH[:, 0:P], ACT.Gelu, bias=b1T[:, u:u + 1], scale=1 / WS
                                       ).then_inc(gelu_done, 1)
                    if early:
                        par, jb = early
                        if i == 1:
                            act.wait_ge(stats, jb + TS)
                            if k >= 2:
                                act.wait_ge(stored, jb)
                            act.copy(acc[par][:, :], psT[:, 0:P]).then_inc(copied, TS)
                        if i == 4:
                            act.wait_ge(xn_ps, jb + TS)
                            act.copy(xnT[0][par][:, :], psT[:, 0:P]).then_inc(xnT_done, TS)
                        if i == 8:
                            act.wait_ge(dl_done, jb + TS)
                            act.activation(ul[:, :], dl[:, :], ACT.Tanh, scale=0.5).then_inc(ul_done, TS)
                    if chain and not first:
                        act.wait_ge(score_ready, n)
                        act.activation(th[p][:, 0:W4, 1], psS[p][:, 0:W4], ACT.Tanh, bias=-K0 / 2, scale=0.5 / WS
                                       ).then_inc(th_ready, 1)
                        act.wait_ge(z_ready, n + 1)
                        act.activation(GF[p][0:NODES, :], Z[p][:, :], ACT.Tanh, bias=half_nodes, scale=half_nodes).then_inc(f_ready, 1)

            over_tiles(act, tile)

        @block.tensor
        def _(pe):
            pe.wait_ge(ld_cst, 16)
            pe.wait_ge(ld_x, 16)
            for g in range(4):
                if g >= 2:
                    pe.wait_ge((xt_sb, xt_sb_act)[g % 2], 1)
                for c in range(4):
                    mm = pe.transpose(bank[g % 2][:, c * P:(c + 1) * P], x_tok[:, 4 * g + c, :], ident)
                mm.then_inc(xt_ps, 1)
            pe.wait_ge(xt_sb, 2)
            pe.wait_ge(xt_sb_act, 2)
            pe.wait_ge(ld_attn, 16 * 9)
            pe.wait_ge(prep, 1)
            for c in range(4):
                if c >= 2:
                    pe.wait_ge(fg_sb, 2 * (c - 1))
                pe.matmul(bank[2 + c % 2][0:48, :], wfg[:, :], xT[:, 2 * c:2 * c + 2, :].rearrange("p b s -> p (b s)"),
                          start=True, stop=True).then_inc(fg_ps, 1)
            for t in range(B * HALF):
                mm = pe.matmul(bank[4][:, t * DH:(t + 1) * DH], xT[:, t // HALF, (t % HALF) * P:(t % HALF + 1) * P],
                               wh[:, :], start=True, stop=True)
            mm.then_inc(hh_ps, 1)
            pe.wait_ge(ld_ffn, 16 * 6)
            pe.transpose(bank[5][:, 0:E], wr_rows[:, :], ident[0:E, 0:E])
            pe.transpose(bank[5][:, 64:64 + UNITS], b1_rows[:, :], ident[0:UNITS, 0:UNITS]).then_inc(wt_ps, 1)
            pe.wait_ge(fg_sb, 8)

            def scores(b):
                if b >= 2:
                    pe.wait_ge(exp_done, 2 * (b - 1))
                for u in range(HALF):
                    mm = pe.matmul(bank[b % 2][:, u * S:(u + 1) * S], fT[:, b, u * P:(u + 1) * P], gT[:, b, :],
                                   start=True, stop=True)
                mm.then_inc(sc_ps, 1)

            def transpose_prob(b):
                pe.wait_ge(pn_done, b + 1)
                if b >= 2:
                    pe.wait_ge(pt_sb, b - 1)
                for j in range(HALF):
                    for u in range(HALF):
                        mm = pe.transpose(bank[2 + b % 2][:, j * S + u * P:j * S + (u + 1) * P],
                                          prob[b % 2][:, u, j * P:(j + 1) * P], ident)
                mm.then_inc(pt_ps, 1)

            def context(b):
                pe.wait_ge(pt_sb, b + 1)
                pe.wait_ge(hh_sb, 1)
                if b >= 1:
                    pe.wait_ge(cx_sb, b)
                for j in range(HALF):
                    mm = pe.matmul(bank[4][0:DH, 0:S], hh[:, HALF * b + j, :], probT[b % 2][:, j, :],
                                   start=(j == 0), stop=(j == HALF - 1))
                mm.then_inc(cx_ps, 1)

            def project_out(b):
                pe.wait_ge(cx_sb, b + 1)
                pe.wait_ge(wt_sb, 1)
                if b >= 1:
                    pe.wait_ge(t1_done, b)
                pe.matmul(bank[5][:, 0:S], wv[:, :], ctxT[b % 2][:, :], start=True, stop=True).then_inc(o_ps, 1)

            def transpose_t1(b):
                pe.wait_ge(t1_done, b + 1)
                if b >= 1:
                    pe.wait_ge(hn_done, 2 * b)
                    pe.wait_ge(bst_done, 2 * b)
                for u in range(HALF):
                    mm = pe.transpose(bank[6][:, u * P:(u + 1) * P], t1T[:, u * P:(u + 1) * P, b], ident)
                mm.then_inc(tk_ps, 1)

            def transpose_h(b):
                pe.wait_ge(hn_done, 2 * (b + 1))
                if b >= 1:
                    pe.wait_ge(ht_done, b)
                    pe.wait_ge(h2_done, b)
                for u in range(HALF):
                    mm = pe.transpose(bank[7][:, u * P:(u + 1) * P], hn[b % 2][:, u, :], ident)
                mm.then_inc(ht_ps, 1)

            for i in range(B + 3):
                if 0 <= i - 1 < B:
                    transpose_prob(i - 1)
                if 0 <= i - 2 < B:
                    transpose_t1(i - 2)
                if i < B:
                    scores(i)
                if 0 <= i - 1 < B:
                    context(i - 1)
                if 0 <= i - 3 < B:
                    transpose_h(i - 3)
                if 0 <= i - 1 < B:
                    project_out(i - 1)

            for done in hpst_loaded:
                pe.wait_ge(done, 16)
            pe.wait_ge(exp_done, 2 * B)
            pe.wait_ge(split, SPLITS)

            PRODUCTS = [(0, 0), (1, 0), (0, 1)]

            def product(out, weight, data, start, stop, which=PRODUCTS):
                for n, (i, j) in enumerate(which):
                    mm = pe.matmul(out, weight[i], data[j], start=(start and n == 0),
                                   stop=(stop and n == len(which) - 1))
                return mm

            w2w, w3w, w13w, vw, nvw = ([t[:, :] for t in w] for w in (w2p, w3p, w13p, vp, nvp))

            def targets(par, i):
                return [hpst[j][par][:, i * B:(i + WIN) * B] for j in range(2)]

            product(psA[1][:, 0:W5], w2w, targets(0, 0), True, True).then_inc(projected, 1)

            def early_work(i, par, jb):
                if i == 0:
                    pe.wait_ge(t2_done, jb + TS)
                    pe.transpose(psT[:, 0:P], t2T[:, :, :].rearrange("p b t -> p (b t)"), ident).then_inc(tok_ps, TS)
                if i == 3:
                    pe.wait_ge(xn_done, jb + TS)
                    pe.transpose(psT[:, 0:P], xn[:, :], ident).then_inc(xn_ps, TS)
                if i == 5:
                    pe.wait_ge(xnT_done, jb + TS)
                    pe.wait_ge(xnT2_done, jb + TS)
                    for n, (i3, j2) in enumerate(PRODUCTS):
                        mm = pe.matmul(psT[:, 0:E], xnT[j2][par][:, :], wrp[i3][:, :], start=(n == 0),
                                       stop=(n == len(PRODUCTS) - 1))
                    mm.then_inc(lg_ps, TS)
                if i == 11:
                    pe.wait_ge(comb_done, jb + TS)
                    pe.transpose(psT[0:E, 0:P], comb[par][:, :], ident).then_inc(ct_ps, TS)
                if i == 13:
                    pe.wait_ge(ct_done, jb + TS)
                    pe.matmul(psT[:, 0:P], combT[:, :], b2s[:, :], start=True, stop=True).then_inc(b2_ps, TS)

            def tile(k, base, steps, chain):
                for i in range(steps):
                    first = k == 0 and i == 0
                    n = base + i
                    p = (i - 1) % 2
                    early, unit, _ = experts_step(k, base, i, k > TILES)
                    par, q = k % 2, i % 2
                    if chain and not first:
                        relu = [bc(Rp[j][p][:, :]) for j in range(2)]
                        pe.wait_ge(r1_ready, n)
                        product(in5(psA[p][:, 0:W5]), w3w, relu, False, False, PRODUCTS[:2])
                        pe.wait_ge(r2_ready, n)
                        product(in5(psA[p][:, 0:W5]), w3w, relu, False, True, PRODUCTS[2:]).then_inc(projected, 1)
                        pe.wait_ge(f_ready, n)
                        pe.wait_ge(g_ready, n)
                        pe.matmul(psS[p][:, 0:W4], fold_w, GF[1 - p][:, :], start=False, stop=False)
                        tanh4 = [Tp[j][p][:, 0:W4] for j in range(2)]
                        pe.wait_ge(t1_ready, n + 1)
                        product(psS[p][:, 0:W4], vw, tanh4, False, False, PRODUCTS[:2])
                    if chain:
                        if i == 0 and k > 0:
                            for done in hpst_loaded:
                                pe.wait_ge(done, base + TS)
                        if first:
                            pe.wait_ge(tf_ready, 1)
                        product(psA[q][:, 0:W5], w2w, targets(par, i + 1), True, False)
                        product(in5(psA[q][:, 0:W5]), w13w, [bc(hpst[j][par][:, i * B:(i + 1) * B]) for j in range(2)],
                                False, False)
                        pe.wait_ge(t2_ready, n + 1)
                    if chain and not first:
                        product(psS[p][:, 0:W4], vw, tanh4, False, True, PRODUCTS[2:]).then_inc(score_ready, 1)
                    if chain:
                        product(psS[q][:, 0:W4], nvw, [Tp[j][1 - q][:, B:W5] for j in range(2)], True, False)
                    _, before, _ = (experts_step(k, base, i - 1, k > TILES) if i else
                                    experts_step(k - 1, base - TS, TS - 1, k - 1 > TILES))
                    if before:
                        pe.wait_ge(gelu_done, before[1] + before[2] + 1)
                    if unit:
                        jp, jb, u = unit
                        if not before:
                            if k == 1 and u == 0:
                                pe.wait_ge(fsplit, 3)
                            else:
                                pe.wait_ge(gelu_done, jb + u)
                        product(psH[:, 0:P], [f1p[m][:, u * P:(u + 1) * P] for m in range(2)],
                                [xnT[m][jp][:, :] for m in range(2)], True, True).then_inc(up_ps, 1)
                    if before:
                        jp, jb, u = before
                        e, half = u // HH, u % HH
                        if half == 0 and not (k == 1 and e < 2):
                            pe.wait_ge(acc_done, jb + 2 * (e - 2) + 2)
                        mm = pe.matmul(psO[e % 2][:, 0:D], hid[u % 2][:, :], f2[:, u, :],
                                       start=(half == 0), stop=(half == HH - 1))
                        if half == HH - 1:
                            mm.then_inc(down_ps, 2)
                    if early:
                        early_work(i, *early)

            over_tiles(pe, tile)

        @block.vector
        def _(dve):
            def split2(whole, to, done):
                dve.tensor_scalar(to[0][:, :], whole, WS, None, ALU.mult).then_inc(split, 1)
                dve.wait_ge(split, done + 1)
                dve.scalar_tensor_tensor(to[1][:, :], whole, WS, to[0][:, :], ALU.mult, ALU.subtract).then_inc(split, 1)
                return done + 2

            dve.memset(wfg[:, DH:32], 0.0)
            dve.wait_ge(ld_w, 16 * 4)
            dve.tensor_copy(vrep[:, :], vcol[:, 0:1].to_broadcast([P, P])).then_inc(prep, 1)
            dve.tensor_tensor(w13[:, :], w1[:, :], w3[:, :], ALU.add).then_inc(prep, 1)
            dve.wait_ge(prep, 2)
            done = 0
            for whole, to in ((w2, w2p), (w3, w3p), (w13, w13p), (vrep, vp)):
                done = split2(whole[:, :], to, done)
            dve.wait_ge(split, done)
            for i in range(2):
                dve.tensor_scalar(nvp[i][:, :], vp[i][:, :], -1.0, None, ALU.mult).then_inc(split, 1)
            done += 2
            dve.wait_ge(xt_ps, 1)
            dve.tensor_copy(xT[:, 0:2, :].rearrange("p b s -> p (b s)"), bank[0][:, :]).then_inc(xt_sb, 1)
            dve.wait_ge(xt_ps, 3)
            dve.tensor_copy(xT[:, 4:6, :].rearrange("p b s -> p (b s)"), bank[0][:, :]).then_inc(xt_sb, 1)
            dve.wait_ge(ld_attn, 16 * 9)
            for c in range(4):
                dve.wait_ge(fg_ps, c + 1)
                for dst, q in ((fT, 0), (gT, 32)):
                    dve.tensor_scalar(dst[:, 2 * c:2 * c + 2, :].rearrange("p b s -> p (b s)"),
                                      bank[2 + c % 2][q:q + DH, :], bfg[q:q + DH, 0:1], None, ALU.add
                                      ).then_inc(fg_sb, 1)
            dve.wait_ge(wt_ps, 1)
            dve.tensor_copy(wrT[:, :], bank[5][:, 0:E]).then_inc(prep, 1)
            dve.tensor_copy(b1T[:, :], bank[5][:, 64:64 + UNITS]).then_inc(wt_sb, 1)
            dve.wait_ge(prep, 3)
            split2(wrT[:, :], wrp, done)

            def row_max(b):
                dve.wait_ge(sc_ps, b + 1)
                if b >= 2:
                    dve.wait_ge(exp_done, 2 * (b - 1))
                dve.tensor_reduce(nmax[b % 2][:, :], bank[b % 2][:, :].rearrange("p (u m) -> p u m", u=HALF),
                                  AX_X, ALU.max, negate=True).then_inc(mx_done, 1)

            def normalise_prob(b):
                dve.wait_ge(exp_done, 2 * (b + 1))
                dve.reciprocal(rsum[b % 2][:, :], esum[b % 2][:, :]).then_inc(rs_done, 1)
                dve.wait_ge(rs_done, b + 1)
                for u in range(HALF):
                    ins = dve.tensor_scalar(prob[b % 2][:, u, :], prob[b % 2][:, u, :], rsum[b % 2][:, u:u + 1], None,
                                            ALU.mult)
                ins.then_inc(pn_done, 1)

            def context(b):
                dve.wait_ge(cx_ps, b + 1)
                if b >= 2:
                    dve.wait_ge(o_ps, b - 1)
                dve.tensor_scalar(ctxT[b % 2][:, :], bank[4][0:DH, 0:S], bhc[:, 0:1], gam[:, 0:1], ALU.add, ALU.mult
                                  ).then_inc(cx_sb, 1)

            def residual(b):
                dve.wait_ge(o_ps, b + 1)
                dve.scalar_tensor_tensor(t1T[:, :, b], bank[5][:, 0:S], bvc[:, 0:1], xT[:, b, :], ALU.add, ALU.add
                                         ).then_inc(t1_done, 1)

            def moments(b):
                dve.wait_ge(tk_ps, b + 1)
                for u in range(HALF):
                    dve.bn_stats(bst[b % 2][:, u, :], bank[6][:, u * P:(u + 1) * P]).then_inc(bst_done, 1)
                dve.wait_ge(bst_done, 2 * (b + 1))
                if b >= 2:
                    dve.wait_ge(bnm_done, b - 1)
                for u in range(HALF):
                    ins = dve.bn_aggr(bmv[b % 2][:, u, :], bst[b % 2][:, u, :])
                ins.then_inc(bmv_done, 1)
                dve.wait_ge(bmv_done, b + 1)
                if b >= 2:
                    dve.wait_ge(brs_done, b - 1)
                dve.tensor_scalar(bve[b % 2][:, :], bmv[b % 2][:, :, 1], EPS, None, ALU.add).then_inc(bve_done, 1)

            def shift(b):
                dve.wait_ge(brs_done, b + 1)
                if b >= 2:
                    dve.wait_ge(hn_done, 2 * (b - 1))
                dve.scalar_tensor_tensor(bnm[b % 2][:, :], bmv[b % 2][:, :, 0], -1.0, brs[b % 2][:, :], ALU.mult,
                                         ALU.mult).then_inc(bnm_done, 1)

            def second_part_h(b):
                dve.wait_ge(ht_ps, b + 1)
                dve.wait_ge(h1_done, b + 1)
                dve.wait_ge(ht_done, b + 1)
                dve.tensor_tensor(hp[1][:, 0:S, b], bank[7][:, 0:S], hp[0][:, 0:S, b], ALU.subtract).then_inc(h2_done, 1)

            for i in range(B + 3):
                if 0 <= i - 2 < B:
                    moments(i - 2)
                if i < B:
                    row_max(i)
                if 0 <= i - 2 < B:
                    shift(i - 2)
                if 0 <= i - 1 < B:
                    context(i - 1)
                if i < B:
                    normalise_prob(i)
                if 0 <= i - 3 < B:
                    second_part_h(i - 3)
                if 0 <= i - 1 < B:
                    residual(i - 1)

            for q in range(2):
                dve.memset(th[q][:, :, 0], 0.0).then_inc(init, 1)
                dve.memset(th[q][:, W4:W5, 1], 1.0).then_inc(init, 1)
                dve.memset(CC[q][:, :, :], 0.0).then_inc(init, 1)
                dve.memset(GF[q][NODES:P, :], 0.0).then_inc(init, 1)
                dve.memset(Z[q][:, :], 1.0).then_inc(z_ready if q == 1 else init, 1)
            dve.memset(Rp[0][0][:, :], 0.0).then_inc(r1_ready, 1)
            dve.memset(Rp[1][0][:, :], 0.0).then_inc(r2_ready, 1)
            dve.wait_ge(init, 9)
            dve.tensor_copy(GF[1][NODES:P, :], g_init[NODES:P, :]).then_inc(g_ready, 1)
            dve.wait_ge(tf_ready, 1)
            dve.wait_ge(t1_ready, 1)
            dve.tensor_tensor(Tp[1][1][:, :], Tf[1][:, :], Tp[0][1][:, :], ALU.subtract).then_inc(t2_ready, 1)
            dve.wait_ge(hst_loaded, 16)
            dve.tensor_copy(ybuf[0][:, 0, :], hst[0][:, 0:B]).then_inc(y_ready, 1)
            for side, ready in ((0, d_ready), (1, e_ready)):
                dve.tensor_scalar(DE[0][:, :, side].rearrange("p (w b) -> p w b", b=B), bc(hst[0][:, 0:B]), 0.5, None,
                                  ALU.mult).then_inc(ready, 1)

            def early_work(i, par, jb, other):
                n = jb + TS
                if i == 0:
                    dve.wait_ge(y_ready, n)
                    t1 = t1T[:, :, :].rearrange("p t b -> p (t b)")[:, bass.ds(jb * B, TS * B)]
                    dve.tensor_tensor(t2T[:, :, :].rearrange("p b t -> p t b"), in5(t1), ybuf[par][:, :, :], ALU.add
                                      ).then_inc(t2_done, TS)
                if i == 1:
                    dve.wait_ge(tok_ps, n)
                    dve.bn_stats(mst[:, :], psT[:, 0:P]).then_inc(stats, TS)
                if i == 2:
                    dve.wait_ge(stats, n)
                    dve.bn_aggr(mmv[:, :], mst[:, :]).then_inc(aggr, TS)
                    other()
                    dve.wait_ge(aggr, n)
                    dve.tensor_scalar(mve[:, :], mmv[:, 1:2], EPS, None, ALU.add).then_inc(ve_done, TS)
                if i == 3:
                    dve.wait_ge(rstd_done, n)
                    dve.wait_ge(copied, n)
                    dve.tensor_scalar(xn[:, :], acc[par][:, :], mmv[:, 0:1], mrs[:, 0:1], ALU.subtract, ALU.mult
                                      ).then_inc(xn_done, TS)
                if i == 5:
                    dve.wait_ge(xnT_done, n)
                    dve.tensor_tensor(xnT[1][par][:, :], psT[:, 0:P], xnT[0][par][:, :], ALU.subtract
                                      ).then_inc(xnT2_done, TS)
                if i == 6:
                    dve.wait_ge(lg_ps, n)
                    dve.scalar_tensor_tensor(lg[:, :], psT[:, 0:E], 1 / WS, brb[:, :], ALU.mult, ALU.add
                                             ).then_inc(lg_done, TS)
                    other()
                    dve.wait_ge(lg_done, n)
                    dve.max(top[:, :], lg[:, :]).then_inc(top_done, TS)
                if i == 7:
                    dve.wait_ge(top_done, n)
                    dve.max_index(topi[:, :], top[:, :], lg[:, :]).then_inc(topi_done, TS)
                    dve.tensor_scalar(dl[:, :], lg[:, :], top[:, 0:1], None, ALU.subtract).then_inc(dl_done, TS)
                if i == 8:
                    dve.wait_ge(topi_done, n)
                    dve.tensor_copy(topf[:, :], topi[:, :]).then_inc(topf_done, TS)
                    other()
                    dve.wait_ge(topf_done, n)
                    dve.tensor_scalar(mask0[:, :], iota8, topf[:, 0:1], None, ALU.is_equal).then_inc(m0_done, TS)
                if i == 9:
                    dve.wait_ge(ul_done, n)
                    dve.tensor_scalar(rl[:, :], ul[:, :], -1.0, 1.0, ALU.mult, ALU.add).then_inc(rl_done, TS)
                    dve.wait_ge(m0_done, n)
                    dve.scalar_tensor_tensor(mask[:, :], iota8, topf[:, 1:2], mask0[:, :], ALU.is_equal, ALU.add
                                             ).then_inc(mask_done, TS)
                    dve.wait_ge(rl_done, n)
                    dve.reciprocal(r2[:, :], rl[:, :]).then_inc(r2_done, TS)
                if i == 10:
                    dve.wait_ge(r2_done, n)
                    dve.scalar_tensor_tensor(el[:, :], ul[:, :], 1.0, r2[:, :], ALU.add, ALU.mult).then_inc(el_done, TS)
                    other()
                    dve.wait_ge(el_done, n)
                    dve.reduce_sum(es[:, :], el[:, :], AX_X).then_inc(es_done, TS)
                if i == 11:
                    dve.wait_ge(es_done, n)
                    dve.reciprocal(ers[:, :], es[:, :]).then_inc(ers_done, TS)
                    dve.wait_ge(ers_done, n)
                    dve.wait_ge(mask_done, n)
                    dve.scalar_tensor_tensor(comb[par][:, :], el[:, :], ers[:, 0:1], mask[:, :], ALU.mult, ALU.mult
                                             ).then_inc(comb_done, TS)
                if i == 13:
                    dve.wait_ge(ct_ps, n)
                    dve.tensor_copy(combT[:, :], psT[0:E, 0:P]).then_inc(ct_done, TS)
                if i == B2_STEP:
                    dve.wait_ge(b2_ps, n)
                    dve.wait_ge(acc_done, jb + 2 * ((i - ACC_LAG + 1) // 2))
                    dve.tensor_tensor(acc[par][:, :], acc[par][:, :], psT[:, 0:P], ALU.add).then_inc(b2_done, TS)

            def mix(p, a, b):
                flat = [t[p][:, a:b, :].rearrange("p c two -> p (c two)") for t in (CC, th, DE)]
                return dve.tensor_tensor_scan(flat[0], flat[1], flat[2], 0.0, ALU.mult, ALU.add)

            def halves(to, frm, side, by):
                return dve.scalar_tensor_tensor(DE[to][:, :, side].rearrange("p (w b) -> p w b", b=B),
                                                CC[frm][:, B:W5 + B, 1].rearrange("p (w b) -> p w b", b=B), by,
                                                bc(yh[:, :]), ALU.mult, ALU.add)

            def add_expert(par, jb, e):
                dve.wait_ge(down_ps, jb + 2 * (e + 1))
                if e == 0:
                    dve.wait_ge(comb_done, jb + TS)
                    dve.wait_ge(copied, jb + TS)
                else:
                    dve.wait_ge(acc_done, jb + 2 * e)
                if e == (B2_STEP + 1 - ACC_LAG) // 2:
                    dve.wait_ge(b2_done, jb + TS)
                dve.scalar_tensor_tensor(acc[par][:, :], psO[e % 2][:, 0:D], comb[par][:, e:e + 1], acc[par][:, :],
                                         ALU.mult, ALU.add).then_inc(acc_done, 2)

            def tile(k, base, steps, chain):
                for i in range(steps):
                    n = base + i
                    p, q = (i - 1) % 2, i % 2
                    early, _, expert = experts_step(k, base, i, k > TILES)
                    if chain and not (k == 0 and i == 0):
                        dve.wait_ge(tf_ready, n + 1)
                        dve.tensor_tensor(Tp[1][p][:, :], Tf[p][:, :], Tp[0][p][:, :], ALU.subtract
                                          ).then_inc(t2_ready, 1)
                        if not (k == 0 and i == 1):
                            halves(p, q, 1, 0.5).then_inc(e_ready, 1)
                    def other():
                        if expert:
                            add_expert(*expert)

                    if early:
                        early_work(i, *early, other)
                    if not (early and i in (2, 6, 8, 10)):
                        other()
                    if chain and not (k == 0 and i == 0):
                        dve.wait_ge(th_ready, n)
                        dve.wait_ge(d_ready, n)
                        dve.wait_ge(e_ready, n)
                        mix(p, 0, B).then_inc(crit_ready, 1)
                        dve.scalar_tensor_tensor(Z[p][:, 0:W4 - B], th[p][0:NODES, B:W4, 1], -1.0,
                                                 th[p][0:NODES, B:W4, 1], ALU.mult, ALU.max).then_inc(z_ready, 1)
                        attended = CC[p][:, 0:B, 1]
                        dve.wait_ge(crit_ready, n)
                        dve.tensor_scalar(Rp[0][q][:, :], attended, 0.0, None, ALU.max).then_inc(r1_ready, 1)
                        dve.tensor_scalar(GF[p][NODES:P, 0:W4 - B], psS[p][NODES:P, B:W4], -K0 * WS, 0.0, ALU.add, ALU.min
                                          ).then_inc(g_ready, 1)
                        dve.wait_ge(r1_ready, n + 1)
                        dve.scalar_tensor_tensor(Rp[1][q][:, :], attended, 0.0, Rp[0][q][:, :], ALU.max, ALU.subtract
                                                 ).then_inc(r2_ready, 1)
                        if i == 0:
                            dve.wait_ge(hst_loaded, base + TS)
                        y = ybuf[k % 2][:, i, :]
                        dve.scalar_tensor_tensor(y, attended, 0.0, hst[k % 2][:, i * B:(i + 1) * B], ALU.max, ALU.add
                                                 ).then_inc(y_ready, 1)
                        mix(p, B, W5).then_inc(c_ready, 1)
                        dve.wait_ge(y_ready, n + 1)
                        dve.tensor_scalar(yh[:, :], y, 0.5, None, ALU.mult).then_inc(yh_ready, 1)
                        dve.wait_ge(c_ready, n)
                        dve.wait_ge(yh_ready, n)
                        halves(q, p, 0, -0.5).then_inc(d_ready, 1)

            over_tiles(dve, tile)


_INS = ["x", "L0_conv_Wf", "L0_conv_bf", "L0_conv_Wg", "L0_conv_bg", "L0_conv_Wh", "L0_conv_bh", "L0_conv_Wv",
        "L0_conv_bv", "L0_conv_gamma", "L1_attn_v", "L1_attn_W1", "L1_attn_W2", "L1_attn_W3", "L1_ffn_Wr",
        "L1_ffn_br", "L1_ffn_W1", "L1_ffn_b1", "L1_ffn_W2", "L1_ffn_b2"]


def kernel(**inputs):
    import numpy as _np
    import concourse.bacc as _bacc
    from concourse import mybir as _mybir
    from concourse.bass_utils import run_bass_kernel_spmd as _run

    nc = _bacc.Bacc("TRN2", target_bir_lowering=False, num_devices=1)
    arrays, args = {}, []
    for name in _INS:
        a = _np.ascontiguousarray(inputs[name])
        arrays[f"in_{name}_dram"] = a
        args.append(nc.dram_tensor(f"in_{name}_dram", a.shape, _mybir.dt.from_np(a.dtype), kind="ExternalInput").ap())
    c = shape_constants()
    arrays["shape_constants_dram"] = c
    args.append(nc.dram_tensor("shape_constants_dram", c.shape, F32, kind="ExternalInput").ap())
    args.append(nc.dram_tensor("out_0_dram", (8, 16, 16, 128), F32, kind="ExternalOutput").ap())
    build(nc, *args)
    r = _run(nc, [arrays], core_ids=[0])
    return r.results[0]["out_0_dram"]
```

```python
from contextlib import ExitStack

import numpy as np

import concourse.bass as bass
from concourse import mybir

F32 = mybir.dt.float32
F16 = mybir.dt.float16
U32 = mybir.dt.uint32
ALU = mybir.AluOpType
ACT = mybir.ActivationFunctionType
AX_X = mybir.AxisListType.X

P = 128
B = 8
S = 256
D = 128
DH = 16
WIN = 5
OLD = WIN - 1
HALF = S // P
TS = 16
TILES = S // TS
E = 8
HID = 256
HH = HID // P
UNITS = E * HH
LEAD = 7
ACC_LAG = 11
W5 = WIN * B
W4 = OLD * B
STG = (TS + WIN) * B
B2_STEP = 14
EPS = 1e-5
WS = 64.0

NODES = 64
NODE_H = (np.log(22.0) - np.log(1e-8)) / (NODES - 1)


def node_constants():
    a = np.exp(np.log(1e-8) + NODE_H * np.arange(NODES)).astype(np.float32)
    h = np.float32(NODE_H)
    return a, h, float(np.sum(float(h) * np.tanh(a.astype(np.float64))))


def shape_constants():
    a, h, _ = node_constants()
    c = np.zeros((P, 2 * P + 1 + E + W4), np.float32)
    c[:, 0:P] = np.eye(P)
    c[0:NODES, P:2 * P] = h * np.float32(WS)
    c[NODES, P:2 * P] = 1.0
    c[0:NODES, 2 * P] = a / 2
    c[:, 2 * P + 1:2 * P + 1 + E] = np.arange(E)
    for j in range(OLD):
        c[:, 2 * P + 1 + E + j * B:2 * P + 1 + E + (j + 1) * B] = -np.log(OLD - j) * WS
    return c


def build(nc, x, Wf, bf, Wg, bg, Wh, bh, Wv, bv, gamma, v, W1, W2, W3, Wr, br, F1, b1, F2, b2, consts, out):
    K0 = node_constants()[2]
    x_tok_dram = x.rearrange("b h w c -> b (h w) c").rearrange("b (u p) c -> p (b u) c", p=P)
    out_dram = out.rearrange("b h w c -> b (h w) c")

    with ExitStack() as ctx:
        def sb(name, shape, dt=F32):
            return ctx.enter_context(nc.sbuf_tensor(name, shape, dt))

        def pair(name, shape, dt=F32):
            return [sb(f"{name}{i}", shape, dt) for i in range(2)]

        def sem(name):
            return ctx.enter_context(nc.semaphore(name))

        bank = [ctx.enter_context(nc.psum_tensor(f"bank{i}", [P, 512], F32)) for i in range(8)]

        cst = sb("cst", [P, 2 * P + 1 + E + W4])
        ident = cst[:, 0:P]
        fold_w = cst[:, P:2 * P]
        half_nodes = cst[0:NODES, 2 * P:2 * P + 1]
        iota8 = cst[:, 2 * P + 1:2 * P + 1 + E]
        g_init = cst[:, 2 * P + 1 + E:]
        w1 = sb("w1", [P, D])
        w2 = sb("w2", [P, D])
        w3 = sb("w3", [P, D])
        w13 = sb("w13", [P, D])
        vcol = sb("vcol", [P, 1])
        vrep = sb("vrep", [P, P])
        def parts(name, n):
            return [sb(f"{name}_{i}", [P, n], F16) for i in range(2)]

        w2p, w3p, w13p, vp, nvp = (parts(n, P) for n in ("w2p", "w3p", "w13p", "vp", "nvp"))
        wrp = parts("wrp", E)
        f1p = parts("f1p", E * HID)
        f1s = sb("f1s", [P, E * HID])
        wfg = sb("wfg", [P, 48])
        wh = sb("wh", [P, DH])
        bfg = sb("bfg", [48, 1])
        bhc = sb("bhc", [DH, 1])
        gam = sb("gam", [DH, 1])
        wv = sb("wv", [DH, P])
        bvc = sb("bvc", [P, 1])
        wr_rows = sb("wr_rows", [E, D])
        wrT = sb("wrT", [P, E])
        brb = sb("brb", [P, E])
        f1 = sb("f1", [P, E, HID])
        f2 = sb("f2", [P, UNITS, D])
        b1_rows = sb("b1_rows", [UNITS, P])
        b1T = sb("b1T", [P, UNITS])
        b2s = sb("b2s", [E, D])
        neghalf = sb("neghalf", [P, HALF])

        x_tok = sb("x_tok", [P, B * HALF, D])
        xT = sb("xT", [P, B, S])
        fT = sb("fT", [DH, B, S])
        gT = sb("gT", [DH, B, S])
        hh = sb("hh", [P, B * HALF, DH])
        nmax = pair("nmax", [P, HALF])
        esum = pair("esum", [P, HALF])
        rsum = pair("rsum", [P, HALF])
        prob = pair("prob", [P, HALF, S])
        probT = pair("probT", [P, HALF, S])
        ctxT = pair("ctxT", [DH, S])
        t1T = sb("t1T", [P, S, B])
        bst = pair("bst", [P, HALF, 6])
        bmv = pair("bmv", [P, HALF, 2])
        bve = pair("bve", [P, HALF])
        brs = pair("brs", [P, HALF])
        bnm = pair("bnm", [P, HALF])
        hn = pair("hn", [P, HALF, D])
        hT = sb("hT", [P, S + WIN, B])
        hp = [sb(f"hp{i}", [P, S + WIN, B], F16) for i in range(2)]

        hst = pair("hst", [P, STG])
        hpst = [pair(f"hpst{i}_", [P, STG], F16) for i in range(2)]
        Tf = pair("Tf", [P, W5])
        Tp = [pair(f"Tp{i}_", [P, W5], F16) for i in range(2)]
        th = pair("th", [P, W5, 2])
        GF = pair("GF", [P, W4])
        Z = pair("Z", [NODES, W4])
        DE = pair("DE", [P, W5, 2])
        CC = pair("CC", [P, W5 + B, 2])
        C16 = pair("C16", [P, B, 2], F16)
        R2 = pair("R2", [P, B], F16)
        yh = sb("yh", [P, B])
        ybuf = pair("ybuf", [P, TS, B])

        t2T = sb("t2T", [P, B, TS])
        acc = pair("acc", [P, D])
        mst = sb("mst", [P, 6])
        mmv = sb("mmv", [P, 2])
        mve = sb("mve", [P, 1])
        mrs = sb("mrs", [P, 1])
        xn = sb("xn", [P, D])
        xnT = [pair(f"xnT{i}_", [P, P], F16) for i in range(2)]
        lg = sb("lg", [P, E])
        top = sb("top", [P, 8])
        topi = sb("topi", [P, 8], U32)
        topf = sb("topf", [P, 8])
        mask0 = sb("mask0", [P, E])
        mask = sb("mask", [P, E])
        dl = sb("dl", [P, E])
        ul = sb("ul", [P, E])
        rl = sb("rl", [P, E])
        el = sb("el", [P, E])
        es = sb("es", [P, 1])
        ers = sb("ers", [P, 1])
        rprob = sb("rprob", [P, E])
        r2 = sb("r2", [P, E])
        comb = pair("comb", [P, E])
        combT = sb("combT", [E, P])
        hid = pair("hid", [P, P])

        psA = bank[0:2]
        psS = bank[2:4]
        psH = bank[4]
        psO = bank[5:7]
        psT = bank[7]

        def hidden(k, u):
            return (psA if k >= TILES and u % 2 else [psH] * 2)[0][:, 0:P]

        ld_cst, ld_w, ld_attn, ld_bias, ld_ffn = (sem(n) for n in ("ld_cst", "ld_w", "ld_attn", "ld_bias", "ld_ffn"))
        ld_x = [sem(f"ld_x{g}") for g in range(4)]
        prep = sem("prep")
        pads, init = sem("pads"), sem("init")
        xt_ps, xt_sb, xt_sb_act, fg_ps, f_sb, g_sb, hh_ps, hh_sb = (
            sem(n) for n in ("xt_ps", "xt_sb", "xt_sb_act", "fg_ps", "f_sb", "g_sb", "hh_ps", "hh_sb"))
        wt_ps, wt_sb = sem("wt_ps"), sem("wt_sb")
        sc_ps, mx_done, exp_done, rs_done, pn_done = (sem(n) for n in ("sc_ps", "mx_done", "exp_done", "rs_done", "pn_done"))
        pt_ps, pt_sb, cx_ps, cx_sb, o_ps, t1_done = (sem(n) for n in ("pt_ps", "pt_sb", "cx_ps", "cx_sb", "o_ps", "t1_done"))
        tk_ps, bst_done, bmv_done, bve_done, brs_done, bnm_done = (
            sem(n) for n in ("tk_ps", "bst_done", "bmv_done", "bve_done", "brs_done", "bnm_done"))
        hn_done, ht_ps, ht_done = sem("hn_done"), sem("ht_ps"), sem("ht_done")

        hst_loaded = sem("hst_loaded")
        hpst_loaded = [sem(f"hpst_loaded{i}") for i in range(2)]
        h1_done, h2_done = sem("h1_done"), sem("h2_done")
        split, fsplit = sem("split"), sem("fsplit")
        projected = sem("projected")
        t1_ready = sem("t1_ready")
        tf_ready = sem("tf_ready")
        t2_ready = sem("t2_ready")
        score_ready = sem("score_ready")
        th_ready = sem("th_ready")
        crit_ready = sem("crit_ready")
        z_ready = sem("z_ready")
        r1_ready = sem("r1_ready")
        r2_ready = sem("r2_ready")
        g_ready = sem("g_ready")
        f_ready = sem("f_ready")
        y_ready = sem("y_ready")
        yh_ready = sem("yh_ready")
        c_ready = sem("c_ready")
        d_ready = sem("d_ready")
        e_ready = sem("e_ready")

        t2_done, tok_ps, copied, stats, aggr, ve_done, rstd_done, xn_done, xn_ps, xnT_done, xnT2_done, lg_ps = (
            sem(n) for n in ("t2_done", "tok_ps", "copied", "stats", "aggr", "ve_done", "rstd_done", "xn_done",
                             "xn_ps", "xnT_done", "xnT2_done", "lg_ps"))
        lg_done, top_done, topi_done, topf_done, m0_done, mask_done, dl_done, ul_done, rl_done, r2_done, el_done = (
            sem(n) for n in ("lg_done", "top_done", "topi_done", "topf_done", "m0_done", "mask_done", "dl_done",
                             "ul_done", "rl_done", "r2_done", "el_done"))
        es_done, ers_done, comb_done, ct_ps, ct_done, b2_ps, b2_done = (
            sem(n) for n in ("es_done", "ers_done", "comb_done", "ct_ps", "ct_done", "b2_ps", "b2_done"))
        prob_done = sem("prob_done")
        up_ps, gelu_done = sem("up_ps"), sem("gelu_done")
        down_ps, acc_done = sem("down_ps"), sem("acc_done")
        stored = sem("stored")

        SPLITS = 4 * 2 + 2 + 2
        block = ctx.enter_context(nc.Block())

        def bc(ap, n=WIN):
            return ap.unsqueeze(1).to_broadcast([P, n, B])

        def in5(ap):
            return ap.rearrange("p (w b) -> p w b", b=B)

        def over_tiles(eng, tile):
            for k in range(2):
                tile(k, TS * k, TS, True)
            with eng.Fori(0, (TILES - 2) // 2) as p:
                base = p * (2 * TS)
                tile(2, base + 2 * TS, TS, True)
                tile(3, base + 3 * TS, TS, True)
            tile(TILES, TS * TILES, TS, False)
            tile(TILES + 1, TS * (TILES + 1), ACC_LAG, False)

        def experts_step(k, base, i, last):
            j, jb = k - 1, base - TS
            j2, jb2 = k - 2, base - 2 * TS
            has, has2 = j >= 0 and not last, j2 >= 0
            unit = expert = None
            if i >= LEAD and has:
                unit = (j % 2, jb, i - LEAD)
            if i < LEAD and has2:
                unit = (j2 % 2, jb2, i - LEAD + UNITS)
            if i >= ACC_LAG and (i - ACC_LAG) % 2 == 0 and has:
                expert = (j % 2, jb, (i - ACC_LAG) // 2)
            if i < ACC_LAG and (i - ACC_LAG) % 2 == 0 and has2 and (i + TS - ACC_LAG) // 2 < E:
                expert = (j2 % 2, jb2, (i + TS - ACC_LAG) // 2)
            return ((j % 2, jb) if has else None), unit, expert

        @block.sync
        def _(sp):
            sp.dma_start(cst[:, :], consts).then_inc(ld_cst, 16)
            for g in range(4):
                sp.dma_start(x_tok[:, 4 * g:4 * g + 4, :], x_tok_dram[:, 4 * g:4 * g + 4, :]).then_inc(ld_x[g], 16)
            for dst, src in ((w1[:, :], W1), (w2[:, :], W2), (w3[:, :], W3), (vcol[:, :], v)):
                sp.dma_start(dst, src).then_inc(ld_w, 16)
            sp.dma_start(brb[:, :], br.partition_broadcast(P)).then_inc(ld_ffn, 16)
            sp.dma_start(wr_rows[:, :], Wr).then_inc(ld_ffn, 16)
            sp.dma_start(b1_rows[:, :], b1.rearrange("e (u p) -> (e u) p", p=P)).then_inc(ld_ffn, 16)
            sp.dma_start(b2s[:, :], b2).then_inc(ld_ffn, 16)
            sp.dma_start(f1[:, :, :], F1.rearrange("e d h -> d e h")).then_inc(ld_ffn, 16)
            sp.dma_start(f2[:, :, :], F2.rearrange("e (u p) d -> p (e u) d", p=P)).then_inc(ld_ffn, 16)
            staged = [(hT, hst, hst_loaded)] + [(hp[i], hpst[i], hpst_loaded[i]) for i in range(2)]

            def load(m, base):
                for src, dst, done in staged:
                    flat = src[:, :, :].rearrange("p t b -> p (t b)")
                    sp.dma_start(dst[m % 2][:, :], flat[:, bass.ds(base * B, STG)]).then_inc(done, 16)

            def reload(m, base):
                sp.wait_ge(th_ready, base - TS + 1)
                load(m, base)

            def store(j, base):
                end = base + TS
                sp.wait_ge(acc_done, end)
                sp.wait_ge(b2_done, end)
                sp.dma_start(out_dram[:, bass.ds(base, TS), :], acc[j % 2][:, :]).then_inc(stored, 16)

            sp.wait_ge(ht_done, B)
            sp.wait_ge(pads, 3)
            sp.wait_ge(h2_done, B)
            load(2, 2 * TS)
            for _, _, done in staged:
                sp.wait_ge(done, 16)
            load(3, 3 * TS)
            with sp.Fori(0, (TILES - 4) // 2) as p:
                base = p * (2 * TS)
                for j in range(2):
                    store(j, base + j * TS)
                    reload(j, base + (j + 4) * TS)
            for j in range(TILES - 4, TILES):
                store(j, j * TS)
            sp.wait_ge(stored, (TILES + 1) * TS)

        @block.gpsimd
        def _(pool):
            for t in [hT] + hp:
                pool.memset(t[:, S:S + WIN, :], 0.0).then_inc(pads, 1)
            pool.memset(neghalf[:, :], -0.5).then_inc(pads, 1)
            pool.dma_start(bhc[:, :], bh.rearrange("(p o) -> p o", o=1)).then_inc(ld_bias, 16)
            pool.dma_start(bvc[:, :], bv.rearrange("(p o) -> p o", o=1)).then_inc(ld_bias, 16)
            pool.dma_start(gam[:, :], gamma.partition_broadcast(DH)).then_inc(ld_bias, 16)
            pool.memset(acc[1][:, :], 0.0).then_inc(stored, TS)
            pool.wait_ge(pads, 4)
            for b in range(B):
                pool.wait_ge(bve_done, b + 1)
                pool.tensor_tensor(brs[b % 2][:, :], bve[b % 2][:, :], neghalf[:, :], ALU.pow).then_inc(brs_done, 1)

            pool.tensor_scalar(f1s[:, :], f1[:, :, :].rearrange("p e h -> p (e h)"), WS, None, ALU.mult).then_inc(fsplit, 1)
            pool.wait_ge(fsplit, 1)
            pool.tensor_copy(f1p[0][:, :], f1s[:, :]).then_inc(fsplit, 1)
            pool.wait_ge(fsplit, 2)
            pool.tensor_tensor(f1p[1][:, :], f1s[:, :], f1p[0][:, :], ALU.subtract).then_inc(fsplit, 1)

            def tile(k, base, steps, chain):
                early, _, _ = experts_step(k, base, 0, k > TILES)
                if early:
                    par, jb = early
                    pool.wait_ge(y_ready, jb + TS)
                    t1 = t1T[:, :, :].rearrange("p t b -> p (t b)")[:, bass.ds(jb * B, TS * B)]
                    pool.tensor_tensor(t2T[:, :, :].rearrange("p b t -> p t b"), in5(t1), ybuf[par][:, :, :], ALU.add
                                       ).then_inc(t2_done, TS)
                    pool.wait_ge(ve_done, jb + TS)
                    pool.tensor_tensor(mrs[:, :], mve[:, :], neghalf[:, 0:1], ALU.pow).then_inc(rstd_done, TS)
                    pool.wait_ge(rstd_done, jb + TS)
                    pool.wait_ge(copied, jb + TS)
                    pool.tensor_scalar(xn[:, :], acc[par][:, :], mmv[:, 0:1], mrs[:, 0:1], ALU.subtract, ALU.mult
                                       ).then_inc(xn_done, TS)
                    pool.wait_ge(ers_done, jb + TS)
                    pool.tensor_scalar(rprob[:, :], el[:, :], ers[:, 0:1], None, ALU.mult).then_inc(prob_done, TS)
                    pool.wait_ge(mask_done, jb + TS)
                    pool.wait_ge(prob_done, jb + TS)
                    pool.tensor_tensor(comb[par][:, :], rprob[:, :], mask[:, :], ALU.mult).then_inc(comb_done, TS)

            over_tiles(pool, tile)

        @block.scalar
        def _(act):
            act.dma_start(wfg[:, 0:DH], Wf).then_inc(ld_attn, 16)
            act.dma_start(wfg[:, 32:32 + DH], Wg).then_inc(ld_attn, 16)
            act.dma_start(bfg[0:DH, :], bf.rearrange("(p o) -> p o", o=1)).then_inc(ld_attn, 16)
            act.dma_start(bfg[32:32 + DH, :], bg.rearrange("(p o) -> p o", o=1)).then_inc(ld_attn, 16)
            act.dma_start(wh[:, :], Wh).then_inc(ld_attn, 16)
            act.dma_start(wv[:, :], Wv).then_inc(ld_attn, 16)
            for g in (1, 3):
                act.wait_ge(xt_ps, g + 1)
                act.copy(xT[:, 2 * g:2 * g + 2, :].rearrange("p b s -> p (b s)"), bank[g][:, :]).then_inc(xt_sb_act, 1)

            def copy_g(c):
                act.wait_ge(ld_attn, 16 * 6)
                act.wait_ge(fg_ps, c + 1)
                act.activation(gT[:, 2 * c:2 * c + 2, :].rearrange("p b s -> p (b s)"), bank[6 + c % 2][32:32 + DH, :],
                               ACT.Identity, bias=bfg[32:32 + DH, 0:1]).then_inc(g_sb, 1)

            def copy_hh():
                act.wait_ge(hh_ps, 1)
                act.copy(hh[:, :, :].rearrange("p i d -> p (i d)"), bank[4][:, 0:B * HALF * DH]).then_inc(hh_sb, 1)

            def exp_rows(b):
                act.wait_ge(mx_done, b + 1)
                if b >= 2:
                    act.wait_ge(pt_ps, b - 1)
                for u in range(HALF):
                    act.activation(prob[b % 2][:, u, :], bank[b % 2][:, u * S:(u + 1) * S], ACT.Exp,
                                   bias=nmax[b % 2][:, u:u + 1], accum_out=esum[b % 2][:, u:u + 1]).then_inc(exp_done, 1)

            def copy_probT(b):
                act.wait_ge(pt_ps, b + 1)
                if b >= 2:
                    act.wait_ge(cx_ps, b - 1)
                act.copy(probT[b % 2][:, :, :].rearrange("p j n -> p (j n)"), bank[2 + b % 2][:, :]).then_inc(pt_sb, 1)

            def normalise(b):
                act.wait_ge(bnm_done, b + 1)
                act.wait_ge(brs_done, b + 1)
                if b >= 2:
                    act.wait_ge(ht_ps, b - 1)
                for u in range(HALF):
                    act.activation(hn[b % 2][:, u, :], bank[6][:, u * P:(u + 1) * P], ACT.Identity,
                                   bias=bnm[b % 2][:, u:u + 1], scale=brs[b % 2][:, u:u + 1]).then_inc(hn_done, 1)

            def copy_hT(b):
                act.wait_ge(ht_ps, b + 1)
                act.copy(hp[0][:, 0:S, b], bank[7][:, 0:S]).then_inc(h1_done, 1)
                act.copy(hT[:, 0:S, b], bank[7][:, 0:S]).then_inc(ht_done, 1)

            copy_g(0)
            for i in range(B + 4):
                if i < 3:
                    copy_g(i + 1)
                if i < B:
                    exp_rows(i)
                if i == B:
                    act.wait_ge(prep, 2)
                    act.activation(ul[:, :], vrep[:, 0:E], ACT.Gelu)
                if i == 1:
                    copy_hh()
                if 0 <= i - 1 < B:
                    copy_probT(i - 1)
                if 0 <= i - 4 < B:
                    copy_hT(i - 4)
                if 0 <= i - 3 < B:
                    normalise(i - 3)

            def tanh_of_item(p):
                act.activation(Tp[0][p][:, :], psA[p][:, 0:W5], ACT.Tanh, scale=1 / WS).then_inc(t1_ready, 1)
                act.activation(Tf[p][:, :], psA[p][:, 0:W5], ACT.Tanh, scale=1 / WS).then_inc(tf_ready, 1)

            act.wait_ge(projected, 1)
            tanh_of_item(1)
            act.wait_ge(z_ready, 1)
            act.activation(GF[1][0:NODES, :], Z[1][:, :], ACT.Tanh, bias=half_nodes, scale=half_nodes).then_inc(f_ready, 1)

            def tile(k, base, steps, chain):
                for i in range(steps):
                    first = k == 0 and i == 0
                    n = base + i
                    p = (i - 1) % 2
                    early, unit, _ = experts_step(k, base, i, k > TILES)
                    if chain and not first:
                        act.wait_ge(projected, n + 1)
                        tanh_of_item(p)
                    if early:
                        par, jb = early
                        if i == 4:
                            act.wait_ge(xn_ps, jb + TS)
                            act.copy(xnT[0][par][:, :], psT[:, 0:P]).then_inc(xnT_done, TS)
                        if i == 8:
                            act.wait_ge(dl_done, jb + TS)
                            act.activation(ul[:, :], dl[:, :], ACT.Tanh, scale=0.5).then_inc(ul_done, TS)
                    if chain and not first:
                        act.wait_ge(score_ready, n)
                        act.activation(th[p][:, 0:W4, 1], psS[p][:, 0:W4], ACT.Tanh, bias=-K0 / 2, scale=0.5 / WS
                                       ).then_inc(th_ready, 1)
                    if early and i == 1:
                        act.wait_ge(stats, jb + TS)
                        if k >= 2:
                            act.wait_ge(stored, jb)
                        act.copy(acc[par][:, :], psT[:, 0:P]).then_inc(copied, TS)
                    if early and i == 8:
                        act.wait_ge(ul_done, jb + TS)
                        act.activation(rl[:, :], ul[:, :], ACT.Identity, bias=1.0, scale=-1.0).then_inc(rl_done, TS)
                    if unit:
                        jp, jb, u = unit
                        act.wait_ge(up_ps, jb + u + 1)
                        act.activation(hid[u % 2][:, :], hidden(k, u), ACT.Gelu, bias=b1T[:, u:u + 1], scale=1 / WS
                                       ).then_inc(gelu_done, 1)
                    if chain and not first:
                        act.wait_ge(z_ready, n + 1)
                        act.activation(GF[p][0:NODES, :], Z[p][:, :], ACT.Tanh, bias=half_nodes, scale=half_nodes).then_inc(f_ready, 1)

            over_tiles(act, tile)

        @block.tensor
        def _(pe):
            pe.wait_ge(ld_cst, 16)
            for g in range(4):
                pe.wait_ge(ld_x[g], 16)
                for c in range(4):
                    mm = pe.transpose(bank[g][:, c * P:(c + 1) * P], x_tok[:, 4 * g + c, :], ident)
                mm.then_inc(xt_ps, 1)

            def project_fg(c):
                pe.wait_ge((xt_sb, xt_sb_act)[c % 2], c // 2 + 1)
                if c == 0:
                    pe.wait_ge(ld_attn, 16 * 6)
                    pe.wait_ge(prep, 1)
                if c >= 2:
                    pe.wait_ge(f_sb, c - 1)
                    pe.wait_ge(g_sb, c - 1)
                pe.matmul(bank[6 + c % 2][0:48, :], wfg[:, :], xT[:, 2 * c:2 * c + 2, :].rearrange("p b s -> p (b s)"),
                          start=True, stop=True).then_inc(fg_ps, 1)

            def project_h():
                pe.wait_ge(xt_sb, 2)
                pe.wait_ge(xt_sb_act, 2)
                for t in range(B * HALF):
                    mm = pe.matmul(bank[4][:, t * DH:(t + 1) * DH],
                                   xT[:, t // HALF, (t % HALF) * P:(t % HALF + 1) * P], wh[:, :], start=True, stop=True)
                mm.then_inc(hh_ps, 1)
                pe.wait_ge(ld_ffn, 16 * 6)
                pe.transpose(bank[5][:, 0:E], wr_rows[:, :], ident[0:E, 0:E])
                pe.transpose(bank[5][:, 64:64 + UNITS], b1_rows[:, :], ident[0:UNITS, 0:UNITS]).then_inc(wt_ps, 1)

            def scores(b):
                pe.wait_ge(f_sb, b // 2 + 1)
                pe.wait_ge(g_sb, b // 2 + 1)
                if b < 2:
                    pe.wait_ge((xt_sb, xt_sb_act)[b], 1)
                if b >= 2:
                    pe.wait_ge(exp_done, 2 * (b - 1))
                for u in range(HALF):
                    mm = pe.matmul(bank[b % 2][:, u * S:(u + 1) * S], fT[:, b, u * P:(u + 1) * P], gT[:, b, :],
                                   start=True, stop=True)
                mm.then_inc(sc_ps, 1)

            def transpose_prob(b):
                pe.wait_ge(pn_done, b + 1)
                if b >= 2:
                    pe.wait_ge(pt_sb, b - 1)
                for j in range(HALF):
                    for u in range(HALF):
                        mm = pe.transpose(bank[2 + b % 2][:, j * S + u * P:j * S + (u + 1) * P],
                                          prob[b % 2][:, u, j * P:(j + 1) * P], ident)
                mm.then_inc(pt_ps, 1)

            def context(b):
                pe.wait_ge(pt_sb, b + 1)
                pe.wait_ge(hh_sb, 1)
                if b >= 1:
                    pe.wait_ge(cx_sb, b)
                for j in range(HALF):
                    mm = pe.matmul(bank[4][0:DH, 0:S], hh[:, HALF * b + j, :], probT[b % 2][:, j, :],
                                   start=(j == 0), stop=(j == HALF - 1))
                mm.then_inc(cx_ps, 1)

            def project_out(b):
                pe.wait_ge(cx_sb, b + 1)
                pe.wait_ge(wt_sb, 1)
                if b >= 1:
                    pe.wait_ge(t1_done, b)
                pe.matmul(bank[5][:, 0:S], wv[:, :], ctxT[b % 2][:, :], start=True, stop=True).then_inc(o_ps, 1)

            def transpose_t1(b):
                pe.wait_ge(t1_done, b + 1)
                if b >= 1:
                    pe.wait_ge(hn_done, 2 * b)
                    pe.wait_ge(bst_done, 2 * b)
                for u in range(HALF):
                    mm = pe.transpose(bank[6][:, u * P:(u + 1) * P], t1T[:, u * P:(u + 1) * P, b], ident)
                mm.then_inc(tk_ps, 1)

            def transpose_h(b):
                pe.wait_ge(hn_done, 2 * (b + 1))
                if b >= 1:
                    pe.wait_ge(ht_done, b)
                    pe.wait_ge(h2_done, b)
                for u in range(HALF):
                    mm = pe.transpose(bank[7][:, u * P:(u + 1) * P], hn[b % 2][:, u, :], ident)
                mm.then_inc(ht_ps, 1)

            project_fg(0)
            for i in range(B + 4):
                if i < 3:
                    project_fg(i + 1)
                if i < B:
                    scores(i)
                if 0 <= i - 3 < B:
                    transpose_t1(i - 3)
                if 0 <= i - 2 < B:
                    context(i - 2)
                if 0 <= i - 4 < B:
                    transpose_h(i - 4)
                if i == 0:
                    project_h()
                if 0 <= i - 1 < B:
                    transpose_prob(i - 1)
                if 0 <= i - 2 < B:
                    project_out(i - 2)

            pe.wait_ge(pads, 3)
            pe.wait_ge(h1_done, B)
            pe.wait_ge(h2_done, B)
            pe.wait_ge(exp_done, 2 * B)
            pe.wait_ge(split, SPLITS)

            PRODUCTS = [(0, 0), (1, 0), (0, 1)]
            ALL_PRODUCTS = PRODUCTS + [(1, 1)]

            def product(out, weight, data, start, stop, which=PRODUCTS):
                for n, (i, j) in enumerate(which):
                    mm = pe.matmul(out, weight[i], data[j], start=(start and n == 0),
                                   stop=(stop and n == len(which) - 1))
                return mm

            w2w, w3w, w13w, vw, nvw = ([t[:, :] for t in w] for w in (w2p, w3p, w13p, vp, nvp))

            def h_parts(k, i, steps):
                if k < 2:
                    return [hp[j][:, k * TS + i:k * TS + i + steps, :].rearrange("p t b -> p (t b)") for j in range(2)]
                return [hpst[j][k % 2][:, i * B:(i + steps) * B] for j in range(2)]

            product(psA[1][:, 0:W5], w2w, h_parts(0, 0, WIN), True, True).then_inc(projected, 1)

            def early_work(i, par, jb):
                if i == 0:
                    pe.wait_ge(t2_done, jb + TS)
                    pe.transpose(psT[:, 0:P], t2T[:, :, :].rearrange("p b t -> p (b t)"), ident).then_inc(tok_ps, TS)
                if i == 3:
                    pe.wait_ge(xn_done, jb + TS)
                    pe.transpose(psT[:, 0:P], xn[:, :], ident).then_inc(xn_ps, TS)
                if i == 5:
                    pe.wait_ge(xnT_done, jb + TS)
                    pe.wait_ge(xnT2_done, jb + TS)
                    for n, (i3, j2) in enumerate(PRODUCTS):
                        mm = pe.matmul(psT[:, 0:E], xnT[j2][par][:, :], wrp[i3][:, :], start=(n == 0),
                                       stop=(n == len(PRODUCTS) - 1))
                    mm.then_inc(lg_ps, TS)
                if i == 11:
                    pe.wait_ge(comb_done, jb + TS)
                    pe.transpose(psT[0:E, 0:P], comb[par][:, :], ident).then_inc(ct_ps, TS)
                if i == 13:
                    pe.wait_ge(ct_done, jb + TS)
                    pe.matmul(psT[:, 0:P], combT[:, :], b2s[:, :], start=True, stop=True).then_inc(b2_ps, TS)

            def tile(k, base, steps, chain):
                for i in range(steps):
                    first = k == 0 and i == 0
                    n = base + i
                    p = (i - 1) % 2
                    early, unit, _ = experts_step(k, base, i, k > TILES)
                    q = i % 2
                    if chain and not first:
                        relu = [bc(C16[p][:, :, 1]), bc(R2[p][:, :])]
                        pe.wait_ge(r1_ready, n)
                        product(in5(psA[p][:, 0:W5]), w3w, relu, False, False, ALL_PRODUCTS[:2])
                        pe.wait_ge(r2_ready, n)
                        product(in5(psA[p][:, 0:W5]), w3w, relu, False, True, ALL_PRODUCTS[2:]).then_inc(projected, 1)
                        if k == 0 and i == 1:
                            pe.wait_ge(t2_ready, 1)
                        product(psS[p][:, 0:W4], nvw, [Tp[j][1 - p][:, B:W5] for j in range(2)], True, False)
                    if chain:
                        if i == 0 and k > 1:
                            for done in hpst_loaded:
                                pe.wait_ge(done, base - TS)
                        if first:
                            pe.wait_ge(tf_ready, 1)
                        product(psA[q][:, 0:W5], w2w, h_parts(k, i + 1, WIN), True, False)
                        product(in5(psA[q][:, 0:W5]), w13w, [bc(h) for h in h_parts(k, i, 1)],
                                False, False)
                    if chain and not first:
                        pe.wait_ge(g_ready, n)
                        pe.wait_ge(f_ready, n)
                        pe.matmul(psS[p][:, 0:W4], fold_w, GF[1 - p][:, :], start=False, stop=False)
                        tanh4 = [Tp[j][p][:, 0:W4] for j in range(2)]
                        pe.wait_ge(t1_ready, n + 1)
                        product(psS[p][:, 0:W4], vw, tanh4, False, False, PRODUCTS[:2])
                        pe.wait_ge(t2_ready, n + 1)
                        product(psS[p][:, 0:W4], vw, tanh4, False, True, PRODUCTS[2:]).then_inc(score_ready, 1)
                    _, before, _ = (experts_step(k, base, i - 1, k > TILES) if i else
                                    experts_step(k - 1, base - TS, TS - 1, k - 1 > TILES))
                    if before and not (k >= TILES and unit):
                        pe.wait_ge(gelu_done, before[1] + before[2] + 1)
                    elif before:
                        pe.wait_ge(gelu_done, before[1] + before[2] + (1 if k == TILES and i == 0 else 0))
                    if unit:
                        jp, jb, u = unit
                        if not before:
                            if k == 1 and u == 0:
                                pe.wait_ge(fsplit, 3)
                            else:
                                pe.wait_ge(gelu_done, jb + u)
                        product(hidden(k, u), [f1p[m][:, u * P:(u + 1) * P] for m in range(2)],
                                [xnT[m][jp][:, :] for m in range(2)], True, True, ALL_PRODUCTS).then_inc(up_ps, 1)
                    if before:
                        jp, jb, u = before
                        e, half = u // HH, u % HH
                        pe.wait_ge(gelu_done, jb + u + 1)
                        if half == 0 and not (k == 1 and e < 2):
                            pe.wait_ge(acc_done, jb + 2 * (e - 2) + 2)
                        mm = pe.matmul(psO[e % 2][:, 0:D], hid[u % 2][:, :], f2[:, u, :],
                                       start=(half == 0), stop=(half == HH - 1))
                        if half == HH - 1:
                            mm.then_inc(down_ps, 2)
                    if early:
                        early_work(i, *early)

            over_tiles(pe, tile)

        @block.vector
        def _(dve):
            def split2(whole, to, done):
                dve.tensor_scalar(to[0][:, :], whole, WS, None, ALU.mult).then_inc(split, 1)
                dve.wait_ge(split, done + 1)
                dve.scalar_tensor_tensor(to[1][:, :], whole, WS, to[0][:, :], ALU.mult, ALU.subtract).then_inc(split, 1)
                return done + 2

            dve.memset(wfg[:, DH:32], 0.0).then_inc(prep, 1)
            for g in (0, 2):
                dve.wait_ge(xt_ps, g + 1)
                dve.tensor_copy(xT[:, 2 * g:2 * g + 2, :].rearrange("p b s -> p (b s)"), bank[g][:, :]).then_inc(xt_sb, 1)
            dve.wait_ge(ld_w, 16 * 4)
            dve.tensor_copy(vrep[:, :], vcol[:, 0:1].to_broadcast([P, P])).then_inc(prep, 1)
            dve.tensor_tensor(w13[:, :], w1[:, :], w3[:, :], ALU.add).then_inc(prep, 1)

            def copy_f(c):
                dve.wait_ge(ld_attn, 16 * 6)
                dve.wait_ge(fg_ps, c + 1)
                dve.tensor_scalar(fT[:, 2 * c:2 * c + 2, :].rearrange("p b s -> p (b s)"), bank[6 + c % 2][0:DH, :],
                                  bfg[0:DH, 0:1], None, ALU.add).then_inc(f_sb, 1)

            copy_f(0)
            def split_weights():
                dve.wait_ge(prep, 3)
                done = 0
                for whole, to in ((w2, w2p), (w3, w3p), (w13, w13p), (vrep, vp)):
                    done = split2(whole[:, :], to, done)
                dve.wait_ge(split, done)
                for i in range(2):
                    dve.tensor_scalar(nvp[i][:, :], vp[i][:, :], -1.0, None, ALU.mult).then_inc(split, 1)
                return done + 2

            def row_max(b):
                dve.wait_ge(sc_ps, b + 1)
                if b >= 2:
                    dve.wait_ge(exp_done, 2 * (b - 1))
                dve.tensor_reduce(nmax[b % 2][:, :], bank[b % 2][:, :].rearrange("p (u m) -> p u m", u=HALF),
                                  AX_X, ALU.max, negate=True).then_inc(mx_done, 1)

            def normalise_prob(b):
                dve.wait_ge(exp_done, 2 * (b + 1))
                dve.reciprocal(rsum[b % 2][:, :], esum[b % 2][:, :]).then_inc(rs_done, 1)
                dve.wait_ge(rs_done, b + 1)
                for u in range(HALF):
                    ins = dve.tensor_scalar(prob[b % 2][:, u, :], prob[b % 2][:, u, :], rsum[b % 2][:, u:u + 1], None,
                                            ALU.mult)
                ins.then_inc(pn_done, 1)

            def context(b):
                dve.wait_ge(ld_bias, 16 * 3)
                dve.wait_ge(cx_ps, b + 1)
                if b >= 2:
                    dve.wait_ge(o_ps, b - 1)
                dve.tensor_scalar(ctxT[b % 2][:, :], bank[4][0:DH, 0:S], bhc[:, 0:1], gam[:, 0:1], ALU.add, ALU.mult
                                  ).then_inc(cx_sb, 1)

            def residual(b):
                dve.wait_ge(o_ps, b + 1)
                dve.scalar_tensor_tensor(t1T[:, :, b], bank[5][:, 0:S], bvc[:, 0:1], xT[:, b, :], ALU.add, ALU.add
                                         ).then_inc(t1_done, 1)

            def moments(b):
                dve.wait_ge(tk_ps, b + 1)
                for u in range(HALF):
                    dve.bn_stats(bst[b % 2][:, u, :], bank[6][:, u * P:(u + 1) * P]).then_inc(bst_done, 1)
                dve.wait_ge(bst_done, 2 * (b + 1))
                if b >= 2:
                    dve.wait_ge(bnm_done, b - 1)
                for u in range(HALF):
                    ins = dve.bn_aggr(bmv[b % 2][:, u, :], bst[b % 2][:, u, :])
                ins.then_inc(bmv_done, 1)
                dve.wait_ge(bmv_done, b + 1)
                if b >= 2:
                    dve.wait_ge(brs_done, b - 1)
                dve.tensor_scalar(bve[b % 2][:, :], bmv[b % 2][:, :, 1], EPS, None, ALU.add).then_inc(bve_done, 1)

            def shift(b):
                dve.wait_ge(brs_done, b + 1)
                if b >= 2:
                    dve.wait_ge(hn_done, 2 * (b - 1))
                dve.scalar_tensor_tensor(bnm[b % 2][:, :], bmv[b % 2][:, :, 0], -1.0, brs[b % 2][:, :], ALU.mult,
                                         ALU.mult).then_inc(bnm_done, 1)

            def second_part_h(b):
                dve.wait_ge(ht_ps, b + 1)
                dve.wait_ge(h1_done, b + 1)
                dve.wait_ge(ht_done, b + 1)
                dve.tensor_tensor(hp[1][:, 0:S, b], bank[7][:, 0:S], hp[0][:, 0:S, b], ALU.subtract).then_inc(h2_done, 1)

            def initial_state():
                for q in range(2):
                    dve.memset(th[q][:, :, 0], 0.0).then_inc(init, 1)
                    dve.memset(th[q][:, W4:W5, 1], 1.0).then_inc(init, 1)
                    dve.memset(CC[q][:, :, :], 0.0).then_inc(init, 1)
                    dve.memset(GF[q][NODES:P, :], 0.0).then_inc(init, 1)
                    dve.memset(Z[q][:, :], 1.0).then_inc(z_ready if q == 1 else init, 1)
                dve.memset(C16[0][:, :, :], 0.0).then_inc(r1_ready, 1)
                dve.memset(R2[0][:, :], 0.0).then_inc(r2_ready, 1)

            for i in range(B + 4):
                if i < 3:
                    copy_f(i + 1)
                if i < B:
                    row_max(i)
                if 0 <= i - 3 < B:
                    moments(i - 3)
                if 0 <= i - 2 < B:
                    context(i - 2)
                if i < B:
                    normalise_prob(i)
                if 0 <= i - 3 < B:
                    shift(i - 3)
                if 0 <= i - 2 < B:
                    residual(i - 2)
                if 0 <= i - 4 < B:
                    second_part_h(i - 4)
                if i == 0:
                    done = split_weights()
                if i == 1:
                    dve.wait_ge(wt_ps, 1)
                    dve.tensor_copy(wrT[:, :], bank[5][:, 0:E]).then_inc(prep, 1)
                    dve.tensor_copy(b1T[:, :], bank[5][:, 64:64 + UNITS]).then_inc(wt_sb, 1)
                    dve.wait_ge(prep, 4)
                    split2(wrT[:, :], wrp, done)
                if i == B + 1:
                    initial_state()

            dve.wait_ge(init, 9)
            dve.tensor_copy(GF[1][NODES:P, :], g_init[NODES:P, :]).then_inc(g_ready, 1)
            dve.wait_ge(tf_ready, 1)
            dve.wait_ge(t1_ready, 1)
            dve.tensor_tensor(Tp[1][1][:, :], Tf[1][:, :], Tp[0][1][:, :], ALU.subtract).then_inc(t2_ready, 1)
            dve.wait_ge(ht_done, B)
            dve.tensor_copy(ybuf[0][:, 0, :], hT[:, 0, :]).then_inc(y_ready, 1)
            for side, ready in ((0, d_ready), (1, e_ready)):
                dve.tensor_scalar(DE[0][:, :, side].rearrange("p (w b) -> p w b", b=B), bc(hT[:, 0, :]), 0.5, None,
                                  ALU.mult).then_inc(ready, 1)

            def early_work(i, par, jb, other):
                n = jb + TS
                if i == 1:
                    dve.wait_ge(tok_ps, n)
                    dve.bn_stats(mst[:, :], psT[:, 0:P]).then_inc(stats, TS)
                if i == 2:
                    dve.wait_ge(stats, n)
                    dve.bn_aggr(mmv[:, :], mst[:, :]).then_inc(aggr, TS)
                    dve.wait_ge(aggr, n)
                    dve.tensor_scalar(mve[:, :], mmv[:, 1:2], EPS, None, ALU.add).then_inc(ve_done, TS)
                if i == 5:
                    dve.wait_ge(xnT_done, n)
                    dve.tensor_tensor(xnT[1][par][:, :], psT[:, 0:P], xnT[0][par][:, :], ALU.subtract
                                      ).then_inc(xnT2_done, TS)
                if i == 6:
                    dve.wait_ge(lg_ps, n)
                    dve.scalar_tensor_tensor(lg[:, :], psT[:, 0:E], 1 / WS, brb[:, :], ALU.mult, ALU.add
                                             ).then_inc(lg_done, TS)
                    dve.wait_ge(lg_done, n)
                    dve.max(top[:, :], lg[:, :]).then_inc(top_done, TS)
                if i == 7:
                    dve.wait_ge(top_done, n)
                    dve.max_index(topi[:, :], top[:, :], lg[:, :]).then_inc(topi_done, TS)
                    dve.tensor_scalar(dl[:, :], lg[:, :], top[:, 0:1], None, ALU.subtract).then_inc(dl_done, TS)
                if i == 8:
                    dve.wait_ge(topi_done, n)
                    dve.tensor_copy(topf[:, :], topi[:, :]).then_inc(topf_done, TS)
                    dve.wait_ge(topf_done, n)
                    dve.tensor_scalar(mask0[:, :], iota8, topf[:, 0:1], None, ALU.is_equal).then_inc(m0_done, TS)
                if i == 9:
                    dve.wait_ge(rl_done, n)
                    dve.reciprocal(r2[:, :], rl[:, :]).then_inc(r2_done, TS)
                    other()
                    dve.wait_ge(r2_done, n)
                    dve.scalar_tensor_tensor(el[:, :], ul[:, :], 1.0, r2[:, :], ALU.add, ALU.mult).then_inc(el_done, TS)
                    dve.wait_ge(m0_done, n)
                    dve.scalar_tensor_tensor(mask[:, :], iota8, topf[:, 1:2], mask0[:, :], ALU.is_equal, ALU.add
                                             ).then_inc(mask_done, TS)
                if i == 10:
                    dve.wait_ge(el_done, n)
                    dve.reduce_sum(es[:, :], el[:, :], AX_X).then_inc(es_done, TS)
                    dve.wait_ge(es_done, n)
                    dve.reciprocal(ers[:, :], es[:, :]).then_inc(ers_done, TS)
                if i == 12:
                    dve.wait_ge(ct_ps, n)
                    dve.tensor_copy(combT[:, :], psT[0:E, 0:P]).then_inc(ct_done, TS)
                if i == B2_STEP:
                    dve.wait_ge(b2_ps, n)
                    dve.wait_ge(acc_done, jb + 2 * ((i - ACC_LAG + 1) // 2))
                    dve.tensor_tensor(acc[par][:, :], acc[par][:, :], psT[:, 0:P], ALU.add).then_inc(b2_done, TS)

            def mix(p, a, b, out=None):
                flat = [t[:, a:b, :].rearrange("p c two -> p (c two)") for t in (out or CC[p], th[p], DE[p])]
                return dve.tensor_tensor_scan(flat[0], flat[1], flat[2], 0.0, ALU.mult, ALU.add)

            def halves(to, frm, side, by):
                return dve.scalar_tensor_tensor(DE[to][:, :, side].rearrange("p (w b) -> p w b", b=B),
                                                CC[frm][:, B:W5 + B, 1].rearrange("p (w b) -> p w b", b=B), by,
                                                bc(yh[:, :]), ALU.mult, ALU.add)

            def add_expert(par, jb, e):
                dve.wait_ge(down_ps, jb + 2 * (e + 1))
                if e == 0:
                    dve.wait_ge(comb_done, jb + TS)
                    dve.wait_ge(copied, jb + TS)
                else:
                    dve.wait_ge(acc_done, jb + 2 * e)
                if e == (B2_STEP + 1 - ACC_LAG) // 2:
                    dve.wait_ge(b2_done, jb + TS)
                dve.scalar_tensor_tensor(acc[par][:, :], psO[e % 2][:, 0:D], comb[par][:, e:e + 1], acc[par][:, :],
                                         ALU.mult, ALU.add).then_inc(acc_done, 2)

            def tile(k, base, steps, chain):
                for i in range(steps):
                    n = base + i
                    p, q = (i - 1) % 2, i % 2
                    early, _, expert = experts_step(k, base, i, k > TILES)
                    if chain and not (k == 0 and i == 0):
                        dve.wait_ge(tf_ready, n + 1)
                        dve.tensor_tensor(Tp[1][p][:, :], Tf[p][:, :], Tp[0][p][:, :], ALU.subtract
                                          ).then_inc(t2_ready, 1)
                        if not (k == 0 and i == 1):
                            halves(p, q, 1, 0.5).then_inc(e_ready, 1)
                    def other():
                        if expert:
                            add_expert(*expert)

                    if early:
                        early_work(i, *early, other)
                    if not (early and i == 9):
                        other()
                    if chain and not (k == 0 and i == 0):
                        dve.wait_ge(th_ready, n)
                        dve.wait_ge(d_ready, n)
                        dve.wait_ge(e_ready, n)
                        mix(p, 0, B, C16[q]).then_inc(r1_ready, 1)
                        mix(p, 0, B).then_inc(crit_ready, 1)
                        dve.scalar_tensor_tensor(Z[p][:, 0:W4 - B], th[p][0:NODES, B:W4, 1], -1.0,
                                                 th[p][0:NODES, B:W4, 1], ALU.mult, ALU.max).then_inc(z_ready, 1)
                        attended = CC[p][:, 0:B, 1]
                        dve.wait_ge(crit_ready, n)
                        dve.wait_ge(r1_ready, n + 1)
                        dve.scalar_tensor_tensor(R2[q][:, :], attended, 0.0, C16[q][:, :, 1], ALU.max, ALU.subtract
                                                 ).then_inc(r2_ready, 1)
                        if i == 0 and k > 1:
                            dve.wait_ge(hst_loaded, base - TS)
                        h = hT[:, k * TS + i, :] if k < 2 else hst[k % 2][:, i * B:(i + 1) * B]
                        y = ybuf[k % 2][:, i, :]
                        dve.scalar_tensor_tensor(y, attended, 0.0, h, ALU.max, ALU.add
                                                 ).then_inc(y_ready, 1)
                        dve.tensor_scalar(GF[p][NODES:P, 0:W4 - B], psS[p][NODES:P, B:W4], -K0 * WS, 0.0, ALU.add, ALU.min
                                          ).then_inc(g_ready, 1)
                        mix(p, B, W5).then_inc(c_ready, 1)
                        dve.wait_ge(y_ready, n + 1)
                        dve.tensor_scalar(yh[:, :], y, 0.5, None, ALU.mult).then_inc(yh_ready, 1)
                        dve.wait_ge(c_ready, n)
                        dve.wait_ge(yh_ready, n)
                        halves(q, p, 0, -0.5).then_inc(d_ready, 1)

            over_tiles(dve, tile)


_INS = ["x", "L0_conv_Wf", "L0_conv_bf", "L0_conv_Wg", "L0_conv_bg", "L0_conv_Wh", "L0_conv_bh", "L0_conv_Wv",
        "L0_conv_bv", "L0_conv_gamma", "L1_attn_v", "L1_attn_W1", "L1_attn_W2", "L1_attn_W3", "L1_ffn_Wr",
        "L1_ffn_br", "L1_ffn_W1", "L1_ffn_b1", "L1_ffn_W2", "L1_ffn_b2"]


def kernel(**inputs):
    import numpy as _np
    import concourse.bacc as _bacc
    from concourse import mybir as _mybir
    from concourse.bass_utils import run_bass_kernel_spmd as _run

    nc = _bacc.Bacc("TRN2", target_bir_lowering=False, num_devices=1)
    arrays, args = {}, []
    for name in _INS:
        a = _np.ascontiguousarray(inputs[name])
        arrays[f"in_{name}_dram"] = a
        args.append(nc.dram_tensor(f"in_{name}_dram", a.shape, _mybir.dt.from_np(a.dtype), kind="ExternalInput").ap())
    c = shape_constants()
    arrays["shape_constants_dram"] = c
    args.append(nc.dram_tensor("shape_constants_dram", c.shape, F32, kind="ExternalInput").ap())
    args.append(nc.dram_tensor("out_0_dram", (8, 16, 16, 128), F32, kind="ExternalOutput").ap())
    build(nc, *args)
    r = _run(nc, [arrays], core_ids=[0])
    return r.results[0]["out_0_dram"]
```
